# Optimizing a Trainium2 kernel written in Bass

```python
import numpy as np
import jax
import jax.numpy as jnp

def _softmax(x, axis=-1):
    return jax.nn.softmax(x, axis=axis)

def _gelu(x):
    return jax.nn.gelu(x, approximate=True)

def _silu(x):
    return jax.nn.silu(x)

def _sigmoid(x):
    return jax.nn.sigmoid(x)

def _layernorm(x, axis=-1, eps=1e-05):
    m = jnp.mean(x, axis=axis, keepdims=True)
    v = jnp.var(x, axis=axis, keepdims=True)
    return (x - m) / jnp.sqrt(v + eps)

def _scatter_add(tgt, idx, src, axis=0):
    return tgt.at[idx].add(src)

def _segment_sum(src, seg, n):
    return jax.ops.segment_sum(src, seg, n)
kernel_name = 'mk_recurrent_d1_jaxref_r4_831326'

def setup_inputs(seed: int=0):
    np.random.seed(seed)
    _w = jnp.asarray

    def _L0_attn_setup():
        import jax, jax.numpy as jnp
        import numpy as np
        from math import sqrt
        EMBED_DIM = 256
        NUM_HEADS = 16
        HEAD_DIM = EMBED_DIM // NUM_HEADS
        CAUSAL = True
        key = jax.random.key(seed)
        ks = jax.random.split(key, 5)
        B, S, E = (2, 512, EMBED_DIM)
        x = jax.random.normal(ks[0], (B, S, E), dtype=jnp.float32)
        scale = 1.0 / sqrt(E)
        Wq = jax.random.normal(ks[1], (E, E), dtype=jnp.float32) * scale
        Wk = jax.random.normal(ks[2], (E, E), dtype=jnp.float32) * scale
        Wv = jax.random.normal(ks[3], (E, E), dtype=jnp.float32) * scale
        Wo = jax.random.normal(ks[4], (E, E), dtype=jnp.float32) * scale
        return {'x': x, 'Wq': Wq, 'Wk': Wk, 'Wv': Wv, 'Wo': Wo}
    _L0_attn_in = _L0_attn_setup()

    def _L0_ffn_setup():
        import jax, jax.numpy as jnp
        import numpy as np
        DIM = 256
        HIDDEN = 768
        SCALE = 1.0 / 127.0

        def _dequant(w_int, dtype):
            return w_int.astype(dtype) * jnp.asarray(SCALE, dtype)
        key = jax.random.key(seed)
        k_x, k_g, k_u, k_d = jax.random.split(key, 4)
        x = jax.random.normal(k_x, (4, 512, DIM), dtype=jnp.float32)
        w_gate = jax.random.randint(k_g, (HIDDEN, DIM), -127, 128, dtype=jnp.int32)
        w_up = jax.random.randint(k_u, (HIDDEN, DIM), -127, 128, dtype=jnp.int32)
        w_down = jax.random.randint(k_d, (DIM, HIDDEN), -127, 128, dtype=jnp.int32)
        return {'x': x, 'w_gate': w_gate, 'w_up': w_up, 'w_down': w_down}
    _L0_ffn_in = _L0_ffn_setup()
    _d = {'L0_attn_x': _L0_attn_in['x'], 'L0_attn_Wq': _L0_attn_in['Wq'], 'L0_attn_Wk': _L0_attn_in['Wk'], 'L0_attn_Wv': _L0_attn_in['Wv'], 'L0_attn_Wo': _L0_attn_in['Wo'], 'L0_ffn_w_gate': _L0_ffn_in['w_gate'], 'L0_ffn_w_up': _L0_ffn_in['w_up'], 'L0_ffn_w_down': _L0_ffn_in['w_down']}
    _x0 = _d['L0_attn_x']
    _d['L0_attn_x'] = jax.random.normal(jax.random.fold_in(jax.random.key(seed), 1), (16, 512, 256), dtype=_x0.dtype)
    del _x0
    return _d

def reference(L0_attn_x, L0_attn_Wq, L0_attn_Wk, L0_attn_Wv, L0_attn_Wo, L0_ffn_w_gate, L0_ffn_w_up, L0_ffn_w_down):

    def _L0_attn_ref(x, Wq, Wk, Wv, Wo):
        import jax, jax.numpy as jnp
        import numpy as np
        from math import sqrt
        EMBED_DIM = 256
        NUM_HEADS = 16
        HEAD_DIM = EMBED_DIM // NUM_HEADS
        CAUSAL = True
        B, S, E = x.shape
        H, D = (NUM_HEADS, HEAD_DIM)

        def proj(W):
            y = jnp.einsum('bse,fe->bsf', x, W)
            return y.reshape(B, S, H, D).transpose(0, 2, 1, 3)
        q, k, v = (proj(Wq), proj(Wk), proj(Wv))
        scores = jnp.einsum('bhsd,bhtd->bhst', q, k)
        if CAUSAL:
            mask = jnp.triu(jnp.ones((S, S), dtype=bool), k=1)
            scores = jnp.where(mask, -jnp.inf, scores)
        attn = jax.nn.softmax(scores / sqrt(D), axis=-1)
        out = jnp.einsum('bhst,bhtd->bhsd', attn, v)
        out = out.transpose(0, 2, 1, 3).reshape(B, S, E)
        return jnp.einsum('bse,fe->bsf', out, Wo)

    def _L0_ffn_ref(x, w_gate, w_up, w_down):
        import jax, jax.numpy as jnp
        import numpy as np
        DIM = 256
        HIDDEN = 768
        SCALE = 1.0 / 127.0

        def _dequant(w_int, dtype):
            return w_int.astype(dtype) * jnp.asarray(SCALE, dtype)
        wg = _dequant(w_gate, x.dtype)
        wu = _dequant(w_up, x.dtype)
        wd = _dequant(w_down, x.dtype)
        gate = jnp.einsum('bsd,hd->bsh', x, wg)
        up = jnp.einsum('bsd,hd->bsh', x, wu)
        h = jax.nn.silu(gate) * up
        return jnp.einsum('bsh,dh->bsd', h, wd)
    x = L0_attn_x
    xn = _layernorm(x, axis=-1)
    s = _L0_attn_ref(xn, L0_attn_Wq, L0_attn_Wk, L0_attn_Wv, L0_attn_Wo)
    g = _silu(_L0_ffn_ref(xn, L0_ffn_w_gate, L0_ffn_w_up, L0_ffn_w_down))
    x = x + s * g
    return x

_drawn_inputs = setup_inputs


def setup_inputs(seed=0):
    import zlib

    import numpy as np

    out = dict(_drawn_inputs(seed))
    spreads = {}
    factors = {}
    for name, (base, spread) in spreads.items():
        noise = np.random.default_rng([zlib.crc32(name.encode()), seed]).standard_normal(out[name].shape)
        drawn = base * np.exp(spread * noise) if base else spread * noise
        out[name] = jnp.asarray(drawn.astype(out[name].dtype))
    for name, factor in factors.items():
        out[name] = (out[name] * factor).astype(out[name].dtype)
    return out
```

```python
import concourse.bass as bass
from concourse import mybir
from contextlib import ExitStack

FP32, F32R, BF16, INT32 = mybir.dt.float32, mybir.dt.float32r, mybir.dt.bfloat16, mybir.dt.int32
ACT = mybir.ActivationFunctionType
ALU = mybir.AluOpType
AX = mybir.AxisListType

P = 128
B, S, E = 16, 512, 256
H = 16
D = E // H
F = 768
KT = E // P
FT = F // P
TT = S // P
PAIRS = H // 2
HALF = 2 * P
ROWS = 3 * D
MROW = ROWS
VW = D + 1
SCALE_W = 1.0 / 127.0
SCALE_S = 1.0 / D ** 0.5
EPS = 1e-5
MASKED = -3.0e38
SEG = [(0,), (1,), (2, 3)]

COUNT = dict(
    f_tr=KT, f_qk=4, f_v=2, f_gu=2 * FT, f_dn=TT, f_op=TT, f_mt=1, f_sm=44, f_st=48, f_pv=12,
    d_ln=3, d_rs=1, d_rc=2, d_xn=1, d_xh=KT, d_xl=KT, d_qh=4, d_ql=4, d_v=2, d_t=2 * FT, d_a=2 * FT, d_h=2 * FT,
    d_hh=2 * FT, d_hl=2 * FT, d_t2=TT, d_g=TT, d_y=TT, d_fin=TT, d_nmh=1, d_nml=1, d_sm=44, d_ex=48,
    d_mk=12, d_ov=4, d_on=2, d_oh=2, d_ol=2)


def maxima_banks():
    banks = []
    for first in (0, PAIRS // 2):
        for parity in (0, 1):
            for i, together in ((0, 4), (1, 2), (2, 1), (3, 1)):
                for j in range(first, first + PAIRS // 2, together):
                    banks.append((i, parity, range(j, j + together)))
    return banks


MAXIMA = maxima_banks()


def merge(a, b):
    out, ta, tb = [], sum(c for c, _ in a), sum(c for c, _ in b)
    i = j = 0
    ca = cb = 0.0
    while i < len(a) or j < len(b):
        if j >= len(b) or (i < len(a) and ca / ta <= cb / tb):
            ca += a[i][0]
            out.append(a[i])
            i += 1
        else:
            cb += b[j][0]
            out.append(b[j])
            j += 1
    return out


def attention_units():
    units = []
    for n in range(13):
        if n < 12:
            for c in range(4):
                units.append(((.22, .16, .22)[n % 3], ("st", 0, 4 * n + c)))
        if n:
            units.append(((1.0, .8, 1.0)[(n - 1) % 3], ("pv", 0, n - 1)))
        if n == 7:
            units.append((0., ("ol", 0, 0)))
        if n == 9:
            units.append((0., ("on", 0, 0)))
    units.append((0., ("ol", 0, 1)))
    return units


def feed_forward_units(half):
    units = []
    for f in range(FT + 1):
        if f < FT:
            units.append((1.3, ("gu", 1, half * FT + f)))
        if f:
            units.append((0., ("hs", 1, half * FT + f - 1)))
    return units + [(2.0, ("dn", 1, 2 * half + j)) for j in range(2)]


def next_batch_units():
    early = [(0., ("ld", 1, 0)), (0., ("ln", 1, 0)), (.5, ("tr", 1, 0)), (.5, ("tr", 1, 1)),
             (1.3, ("qk", 1, 0)), (1.3, ("qk", 1, 1)), (1.3, ("v", 1, 0)), (0., ("ls", 1, 0)),
             (1.3, ("qk", 1, 2)), (1.3, ("qk", 1, 3)), (1.3, ("v", 1, 1)), (0., ("ls", 1, 1))]
    ffn = feed_forward_units(0)
    maxima = [(.3, ("sm", 1, k)) for k in range(len(MAXIMA))]
    return early + ffn[:5] + merge(ffn[5:], maxima)


def tail_units(current, following):
    units = [(0., ("mt", 1, 0))] + feed_forward_units(1) if following else []
    if current:
        at = min(11, len(units))
        units[at:at] = [(0., ("on", 0, 1))]
        units += [(.7, ("op", 0, j)) for j in range(TT)]
    return units


def schedule(current, following):
    a = attention_units() if current else []
    b = next_batch_units() if following else []
    if a and b:
        a = a[:8] + merge(a[8:], b[2:])
        a[0:0] = b[:2]
    else:
        a = a + b
    units, n = [], 0
    for _, u in a + tail_units(current, following):
        bank = None
        if u[0] in ("tr", "qk", "v", "gu", "dn", "op", "mt"):
            bank = n % 3
            n += 1
        units.append((*u, bank))
    return units


RELEASED = dict(tr="d_xl", qk="d_ql", v="d_v", gu="d_h", dn="d_g", op="d_y", mt="d_nml")


def build(nc, x, wqT, wkT, wvT, woT, wgT, wuT, wdT, out, scratch_qk, scratch_o):
    with ExitStack() as ctx:
        def sb(name, shape, dt=FP32):
            return ctx.enter_context(nc.sbuf_tensor(name, shape, dt))

        def bank(name):
            return ctx.enter_context(nc.psum_tensor(name, [P, 512], FP32))

        def sem(name):
            return ctx.enter_context(nc.semaphore(name))

        W = {w: [sb(f"w{w}_{part}", [P, k, n]) for part in ("hi", "lo")]
             for w, k, n in (("k", KT, E), ("q", KT, E), ("v", KT, E), ("g", KT, F), ("u", KT, F), ("d", FT, E), ("o", KT, E))}
        X = [sb(f"x{i}", [P, TT, E]) for i in range(2)]
        XN = sb("xn", [P, TT, E])
        STATS = sb("stats", [P, TT, 6])
        MV = sb("mv", [P, TT, 2])
        VAR = sb("var", [P, TT])
        RSTD = sb("rstd", [P, TT])
        MINUS_HALF = sb("minus_half", [P, TT])
        XT = [sb(f"xt_{part}", [P, KT, S]) for part in ("hi", "lo")]
        QKP = [sb(f"qk_{part}", [P, 2, S]) for part in ("hi", "lo")]
        QS = [sb(f"q_stack{i}", [P, PAIRS, S]) for i in range(2)]
        KS = [sb(f"k_stack{i}", [P, PAIRS, S]) for i in range(2)]
        V = [sb(f"v{i}", [P, TT, H, VW]) for i in range(2)]
        MX = sb("row_max", [P, 64])
        NM = [sb(f"neg_max_{part}", [64, P]) for part in ("hi", "lo")]
        PR = sb("probs", [P, 2, 4, 512])
        O = sb("o", [P, 2, S])
        OC = sb("o_compact", [P, S])
        DEN = sb("o_sums", [P, S])
        OT = [sb(f"o_{part}", [P, KT, S]) for part in ("hi", "lo")]
        T = sb("tanh", [P, 2, HALF])
        HF = sb("h", [P, 2, HALF])
        HT = [sb(f"h_{part}", [P, FT, HALF]) for part in ("hi", "lo")]
        T2 = sb("tanh_out", [P, E])
        GATES = sb("gates", [P, 2, TT, E])
        G = [GATES[:, i, :, :] for i in range(2)]
        Y = sb("y", [P, 2, E])
        IDF = sb("identity", [P, P])
        IDB = sb("identity_bf16", [P, P], BF16)
        MASK = sb("causal_mask", [P, 4, P], BF16)
        ZERO = sb("zeros", [P, 512], BF16)

        MISC = [bank(f"misc{i}") for i in range(3)]
        SMB = [bank(f"maxima{i}") for i in range(2)]
        STB = [bank(f"scores{i}") for i in range(2)]
        PVB = bank("values")

        sems = {name: sem(name) for name in COUNT}
        s_const, s_fixed, s_passed = sem("s_const"), sem("s_fixed"), sem("s_passed")
        s_w = {w: sem(f"s_w{w}") for w in W}
        c_wf, c_wh, c_wl = sem("c_wf"), sem("c_wh"), sem("c_wl")
        s_x, s_out, s_m = sem("s_x"), sem("s_out"), sem("s_m")
        s_qkst = [sem(f"s_qkst{i}") for i in range(2)]
        s_stack = {w: sem(f"s_stack_{w}") for w in "kq"}
        s_ost = [sem(f"s_ost{i}") for i in range(2)]
        s_oc = [sem(f"s_oc{i}") for i in range(2)]

        def r(ap):
            return ap.bitcast(F32R)

        def nth(name, beta, k):
            return beta * COUNT[name] + k + 1

        def wait(e, s, value, apart=False):
            if isinstance(value, int) and value <= 0:
                return
            e.wait_ge(s, value)
            if (apart or e is nc.sync) and not isinstance(value, int):
                e.sem_inc(s_passed, 1)

        def after(e, name, beta, k, apart=False):
            wait(e, sems[name], nth(name, beta, k), apart)

        def signal(ins, name):
            ins.then_inc(sems[name], 1)

        def parts_product(dst, lhs, rhs, start, stop):
            todo = [(0, 0), (0, 1), (1, 0)]
            for j, (a, b) in enumerate(todo):
                last = nc.tensor.matmul(dst, r(lhs[a]), r(rhs[b]), start=start and j == 0, stop=stop and j == 2)
            return last

        def u_ld(en, e, beta, par, k, bank, prev):
            if en == "sp":
                wait(e, s_out, 32 * (beta - 1))
                e.dma_start(X[par][:], x[beta].rearrange("(t p) e -> p t e", p=P)).then_inc(s_x, 16)

        def u_ln(en, e, beta, par, k, bank, prev):
            if en == "dve":
                wait(e, s_x, 16 * (beta + 1))
                for t in range(TT):
                    last = e.bn_stats(STATS[:, t, :], X[par][:, t, :])
                signal(last, "d_ln")
                after(e, "d_ln", beta, 0, apart=True)
                for t in range(TT):
                    last = e.bn_aggr(MV[:, t, :], STATS[:, t, :])
                signal(last, "d_ln")
                after(e, "d_ln", beta, 1)
                signal(e.tensor_scalar_add(VAR[:], MV[:, :, 1], EPS), "d_ln")
                after(e, "d_rs", beta, 0)
                after(e, "f_tr", beta - 1, KT - 1)
                for t in range(TT):
                    last = e.tensor_scalar(XN[:, t, :], X[par][:, t, :], MV[:, t, 0:1], RSTD[:, t:t + 1],
                                           ALU.subtract, ALU.mult)
                signal(last, "d_xn")
            elif en == "pool":
                after(e, "d_ln", beta, 2)
                signal(e.tensor_tensor(RSTD[:], VAR[:], MINUS_HALF[:], ALU.pow), "d_rs")

        def u_tr(en, e, beta, par, k, bank, prev):
            if en == "pe":
                after(e, "d_xn", beta, 0)
                prev(e)
                for t in range(TT):
                    last = e.transpose(bank[:, t * P:(t + 1) * P], XN[:, t, k * P:(k + 1) * P], IDF[:])
                signal(last, "f_tr")
            elif en == "act":
                after(e, "f_tr", beta, k)
                signal(e.activation(r(XT[0][:, k, :]), bank[:], ACT.Copy), "d_xh")
            elif en == "dve":
                after(e, "d_xh", beta, k)
                signal(e.tensor_tensor(r(XT[1][:, k, :]), bank[:], XT[0][:, k, :], ALU.subtract), "d_xl")

        def u_qk(en, e, beta, par, k, bank, prev):
            w, m = "kkqq"[k], k % 2
            if en == "pe":
                after(e, "d_xl", beta, KT - 1)
                prev(e)
                for t in range(KT):
                    last = parts_product(bank[:], [part[:, t, m * P:(m + 1) * P] for part in W[w]],
                                         [part[:, t, :] for part in XT], t == 0, t == KT - 1)
                signal(last, "f_qk")
            elif en == "act":
                after(e, "f_qk", beta, k)
                wait(e, s_qkst[m], 64 * beta + 32 * (k // 2))
                signal(e.activation(r(QKP[0][:, m, :]), bank[:], ACT.Copy), "d_qh")
            elif en == "dve":
                after(e, "d_qh", beta, k)
                signal(e.tensor_tensor(r(QKP[1][:, m, :]), bank[:], QKP[0][:, m, :], ALU.subtract), "d_ql")
            elif en == "sp":
                wait(e, s_stack[w], 96 * beta)
                after(e, "d_ql", beta, k)
                for part in range(2):
                    e.dma_start(scratch_qk[k // 2, part, m * P:(m + 1) * P, :], QKP[part][:, m, :])\
                     .then_inc(s_qkst[m], 16)

        def u_ls(en, e, beta, par, k, bank, prev):
            if en == "sp":
                for m in range(2):
                    wait(e, s_qkst[m], 64 * beta + 32 * (k + 1))
                stack, order = ((KS[par], (0, 0, 1)), (QS[par], (0, 1, 0)))[k]
                for slot, part in enumerate(order):
                    rows = scratch_qk[k, part].rearrange("(pair parity d) s -> parity d pair s", parity=2, d=D)
                    for parity in range(2):
                        at = 64 * parity + D * slot
                        e.dma_start(stack[at:at + D, :, :], rows[parity]).then_inc(s_stack["kq"[k]], 16)

        def u_v(en, e, beta, par, k, bank, prev):
            if en == "pe":
                prev(e)
                for j in range(2):
                    t = 2 * k + j
                    for kt in range(KT):
                        last = parts_product(bank[:, j * E:(j + 1) * E], [part[:, kt, t * P:(t + 1) * P] for part in XT],
                                             [part[:, kt, :] for part in W["v"]], kt == 0, kt == KT - 1)
                signal(last, "f_v")
            elif en == "act":
                after(e, "f_v", beta, k)
                for j in range(2):
                    last = e.activation(V[par][:, 2 * k + j, :, 0:D],
                                        bank[:, j * E:(j + 1) * E].rearrange("p (h d) -> p h d", d=D), ACT.Copy)
                signal(last, "d_v")

        def u_gu(en, e, beta, par, k, bank, prev):
            half, f = divmod(k, FT)
            slot = k % 2
            if en == "pe":
                prev(e)
                for j, w in enumerate("gu"):
                    for kt in range(KT):
                        last = parts_product(bank[:, j * HALF:(j + 1) * HALF],
                                             [part[:, kt, f * P:(f + 1) * P] for part in W[w]],
                                             [part[:, kt, half * HALF:(half + 1) * HALF] for part in XT],
                                             kt == 0, kt == KT - 1)
                signal(last, "f_gu")
            elif en == "act":
                after(e, "f_gu", beta, k)
                after(e, "d_h", beta, k - 2)
                signal(e.activation(T[:, slot, :], bank[:, 0:HALF], ACT.Tanh, scale=0.5 * SCALE_W), "d_t")
            elif en == "dve":
                after(e, "d_t", beta, k)
                signal(e.scalar_tensor_tensor(out=T[:, slot, :], in0=T[:, slot, :], scalar=1.0, in1=bank[:, 0:HALF],
                                              op0=ALU.add, op1=ALU.mult), "d_a")
                after(e, "d_a", beta, k)
                after(e, "d_hl", beta, k - 2)
                signal(e.scalar_tensor_tensor(out=HF[:, slot, :], in0=bank[:, HALF:2 * HALF],
                                              scalar=0.5 * SCALE_W * SCALE_W, in1=T[:, slot, :],
                                              op0=ALU.mult, op1=ALU.mult), "d_h")

        def u_hs(en, e, beta, par, k, bank, prev):
            f, slot = k % FT, k % 2
            if en == "act":
                after(e, "d_h", beta, k)
                signal(e.activation(r(HT[0][:, f, :]), HF[:, slot, :], ACT.Copy), "d_hh")
            elif en == "pool":
                after(e, "d_hh", beta, k)
                signal(e.tensor_tensor(r(HT[1][:, f, :]), HF[:, slot, :], HT[0][:, f, :], ALU.subtract), "d_hl")

        def u_dn(en, e, beta, par, k, bank, prev):
            half, j = divmod(k, 2)
            if en == "pe":
                after(e, "d_hl", beta, half * FT + FT - 1)
                prev(e)
                for f in range(FT):
                    last = parts_product(bank[:, 0:E], [part[:, f, j * P:(j + 1) * P] for part in HT],
                                         [part[:, f, :] for part in W["d"]], f == 0, f == FT - 1)
                signal(last, "f_dn")
            elif en == "act":
                after(e, "f_dn", beta, k)
                after(e, "d_g", beta, k - 1)
                signal(e.activation(T2[:], bank[:, 0:E], ACT.Tanh, scale=0.5 * SCALE_W), "d_t2")
            elif en == "dve":
                after(e, "d_t2", beta, k)
                signal(e.scalar_tensor_tensor(out=G[par][:, k, :], in0=T2[:], scalar=1.0, in1=bank[:, 0:E],
                                              op0=ALU.add, op1=ALU.mult), "d_g")

        def u_sm(en, e, beta, par, k, bank, prev):
            i, parity, pairs = MAXIMA[k]
            keys, n = P * (i + 1), len(pairs)
            low = 64 * parity
            scores = SMB[k % 2][:, 0:n * keys].rearrange("p (n t) -> p n t", n=n)
            if en == "pe":
                if k == 0:
                    for w in "kq":
                        wait(e, s_stack[w], 96 * (beta + 1))
                after(e, "d_sm", beta, k - 2)
                for j, pair in enumerate(pairs):
                    nc.tensor.matmul(scores[:, j, :], r(QS[par][low:low + ROWS, pair, i * P:(i + 1) * P]),
                                     r(KS[par][low:low + ROWS, pair, 0:keys]), start=j == 0, stop=False,
                                     skip_group_check=True)
                last = nc.tensor.matmul(scores[:, :, i * P:keys], IDB[:], MASK[:, 0:n, :], start=False, stop=True,
                                        skip_group_check=True)
                signal(last, "f_sm")
            elif en == "dve":
                after(e, "f_sm", beta, k)
                at = parity * 32 + pairs[0] * 4 + i
                signal(e.tensor_reduce(MX[:, at:at + 4 * (n - 1) + 1:4], scores, axis=AX.X, op=ALU.max), "d_sm")

        def u_mt(en, e, beta, par, k, bank, prev):
            if en == "pe":
                prev(e)
                after(e, "d_sm", beta, len(MAXIMA) - 1, apart=True)
                signal(e.transpose(bank[0:64, 0:P], MX[:], IDF[:]), "f_mt")
            elif en == "act":
                after(e, "f_mt", beta, 0)
                wait(e, s_m, 64 * beta)
                signal(e.activation(r(NM[0][:]), bank[0:64, 0:P], ACT.Copy, scale=-1.0), "d_nmh")
            elif en == "dve":
                after(e, "d_nmh", beta, 0)
                signal(e.scalar_tensor_tensor(out=r(NM[1][:]), in0=bank[0:64, 0:P], scalar=-1.0, in1=NM[0][:],
                                              op0=ALU.mult, op1=ALU.subtract), "d_nml")
            elif en == "sp":
                after(e, "d_nml", beta, 0)
                for parity in range(2):
                    for part in range(2):
                        row = 64 * parity + MROW + part
                        e.dma_start(QS[par][row:row + 1, :, :].rearrange("o a (i s) -> o (a i) s", i=TT),
                                    NM[part][32 * parity:32 * parity + 32, :]).then_inc(s_m, 16)

        def segment_offsets(seg):
            at = 0
            for j in SEG[seg]:
                yield j, at, S - j * P
                at += S - j * P

        def u_st(en, e, beta, par, k, bank, prev):
            g, rest = divmod(k, 12)
            seg, c = divmod(rest, 4)
            n = 3 * g + seg
            head = 4 * g + c
            low, pair = 64 * (head % 2), head // 2
            width = sum(w for _, _, w in segment_offsets(seg))
            if en == "pe":
                if k == 0:
                    wait(e, s_m, 64 * (beta + 1))
                after(e, "d_ex", beta, k - 2)
                for j, at, w in segment_offsets(seg):
                    last = nc.tensor.matmul(STB[k % 2][:, at:at + w], r(KS[par][low:low + ROWS + 2, pair, j * P:(j + 1) * P]),
                                            r(QS[par][low:low + ROWS + 2, pair, j * P:S]), start=True, stop=True)
                signal(last, "f_st")
            elif en == "act":
                if c == 0:
                    after(e, "f_pv", beta, n - 2)
                after(e, "f_st", beta, k)
                signal(e.activation(PR[:, n % 2, c, 0:width], STB[k % 2][:, 0:width], ACT.Exp, scale=SCALE_S), "d_ex")
            elif en == "pool" and c == 3:
                after(e, "d_ex", beta, k, apart=True)
                tiles = len(SEG[seg])
                diag = PR[:, n % 2, :, :].rearrange("p c (b s) -> p c b s", s=HALF)[:, :, 0:tiles, 0:P]
                signal(e.affine_select(out=diag, in_=diag, compare_op=ALU.is_ge, fill=0.0, base=0,
                                       pattern=[[0, 4], [0, tiles], [1, P]], channel_multiplier=-1), "d_mk")

        def u_pv(en, e, beta, par, k, bank, prev):
            g, seg = divmod(k, 3)
            if en == "pe":
                if k == 0:
                    after(e, "d_v", beta, 1)
                if seg == 0:
                    after(e, "d_ov", beta, g - 1)
                after(e, "d_mk", beta, k)
                for j, at, w in segment_offsets(seg):
                    for c in range(4):
                        last = nc.tensor.matmul(PVB[32 * c:32 * c + VW, j * P:S], V[par][:, j, 4 * g + c, :],
                                                PR[:, k % 2, c, at:at + w], start=j == 0, stop=j == TT - 1)
                signal(last, "f_pv")
            elif en == "act" and seg == 2:
                wait(e, s_ost[g % 2], 32 * beta + 16 * (g // 2))
                after(e, "f_pv", beta, k)
                signal(e.activation(O[:, g % 2, :], PVB[:], ACT.Copy), "d_ov")
            elif en == "sp" and seg == 2:
                wait(e, s_oc[g // 2], 32 * beta)
                after(e, "d_ov", beta, g)
                e.dma_start(scratch_o[g * P:(g + 1) * P, :], O[:, g % 2, :]).then_inc(s_ost[g % 2], 16)

        def u_ol(en, e, beta, par, k, bank, prev):
            if en == "sp":
                for m in range(2):
                    wait(e, s_ost[m], 32 * beta + 16 * (k + 1))
                after(e, "d_ol", beta, k - 1)
                rows = scratch_o[k * 2 * P:(k + 1) * 2 * P, :].rearrange("(h r) s -> h r s", r=32)
                e.dma_start(OC[:], rows[:, 0:D, :]).then_inc(s_oc[k], 16)
                e.dma_start(DEN[:], rows[:, D:D + 1, :].to_broadcast([8, D, S])).then_inc(s_oc[k], 16)

        def u_on(en, e, beta, par, k, bank, prev):
            if en == "dve":
                wait(e, s_oc[k], 32 * (beta + 1))
                signal(e.reciprocal(DEN[:], DEN[:]), "d_rc")
                after(e, "d_rc", beta, k)
                signal(e.tensor_tensor(OC[:], OC[:], DEN[:], ALU.mult), "d_on")
                after(e, "d_oh", beta, k)
                signal(e.tensor_tensor(r(OT[1][:, k, :]), OC[:], OT[0][:, k, :], ALU.subtract), "d_ol")
            elif en == "act":
                after(e, "d_on", beta, k)
                signal(e.activation(r(OT[0][:, k, :]), OC[:], ACT.Copy), "d_oh")

        def u_op(en, e, beta, par, k, bank, prev):
            if en == "pe":
                after(e, "d_ol", beta, 1)
                prev(e)
                for kt in range(KT):
                    last = parts_product(bank[:, 0:E], [part[:, kt, k * P:(k + 1) * P] for part in OT],
                                         [part[:, kt, :] for part in W["o"]], kt == 0, kt == KT - 1)
                signal(last, "f_op")
            elif en == "dve":
                after(e, "f_op", beta, k)
                after(e, "d_fin", beta, k - 2)
                signal(e.scalar_tensor_tensor(out=Y[:, k % 2, :], in0=bank[:, 0:E], scalar=0.5 * SCALE_W, in1=G[par][:, k, :],
                                              op0=ALU.mult, op1=ALU.mult), "d_y")
                after(e, "d_y", beta, k)
                signal(e.tensor_tensor(X[par][:, k, :], Y[:, k % 2, :], X[par][:, k, :], ALU.add), "d_fin")
            elif en == "sp" and k % 2:
                after(e, "d_fin", beta, k)
                e.dma_start(out[beta].rearrange("(t p) e -> p t e", p=P)[:, k - 1:k + 1, :],
                            X[par][:, k - 1:k + 1, :]).then_inc(s_out, 16)

        UNIT = dict(ld=u_ld, ln=u_ln, tr=u_tr, qk=u_qk, ls=u_ls, v=u_v, gu=u_gu, hs=u_hs, dn=u_dn, sm=u_sm,
                    mt=u_mt, st=u_st, pv=u_pv, ol=u_ol, on=u_on, op=u_op)

        def step(en, e, b, parity, units, users):
            for kind, ahead, k, n in units:
                def prev(e, n=n):
                    if n in users:
                        last, last_ahead, last_k = users[n]
                        after(e, RELEASED[last], b + last_ahead, last_k)
                UNIT[kind](en, e, b + ahead, (parity + ahead) % 2, k, None if n is None else MISC[n], prev)
                if n is not None:
                    users[n] = (kind, ahead, k)
            return {n: (kind, ahead - 1, k) for n, (kind, ahead, k) in users.items()}

        def run(en, e):
            users = step(en, e, -1, 1, schedule(False, True), {})
            if en in ("act", "sp"):
                wait(e, c_wl, len(W))
            steady = schedule(True, True)
            users = step(en, e, 0, 0, steady, users)
            with e.Fori(0, (B - 2) // 2) as pair:
                b = 2 * pair + 1
                after_one = step(en, e, b, 1, steady, dict(users))
                step(en, e, b + 1, 0, steady, dict(after_one))
            step(en, e, B - 1, 1, schedule(True, False), users)

        stage_p = PR[:].rearrange("p a b c -> p (a b c)")
        stage_g = GATES[:].rearrange("p a t e -> p (a t e)")
        WEIGHTS = [
            ("k", wkT, stage_p[:, 0:512], 0), ("q", wqT, stage_p[:, 512:1024], 0), ("v", wvT, stage_p[:, 1024:1536], 0),
            ("g", wgT, stage_p[:, 1536:3072], 0), ("u", wuT, stage_g[:, 0:1536], 0),
            ("o", woT, stage_p[:, 3072:3584], 0), ("d", wdT, stage_p[:, 0:1536], 3)]

        block = ctx.enter_context(nc.Block())

        @block.gpsimd
        def _(e):
            e.memset(IDF[:], 0.0).then_inc(s_const, 1)
            e.memset(IDB[:], 0.0).then_inc(s_const, 1)
            e.memset(MASK[:], 0.0).then_inc(s_const, 1)
            e.memset(ZERO[:], 0.0).then_inc(s_const, 1)
            e.memset(MINUS_HALF[:], -0.5).then_inc(s_const, 1)
            e.wait_ge(s_const, 5)
            for m in (IDF, IDB):
                e.affine_select(out=m[:], in_=m[:], compare_op=ALU.not_equal, fill=1.0, base=0,
                                pattern=[[-1, P]], channel_multiplier=1).then_inc(s_const, 1)
            e.affine_select(out=MASK[:], in_=MASK[:], compare_op=ALU.is_ge, fill=MASKED, base=0,
                            pattern=[[0, 4], [-1, P]], channel_multiplier=1).then_inc(s_const, 1)
            for stack in KS:
                e.memset(stack[:], 1.0).then_inc(s_const, 1)
            for v in V:
                e.memset(v[:], 1.0).then_inc(s_const, 1)
            run("pool", e)

        @block.sync
        def _(e):
            for w, src, stage, free in WEIGHTS:
                wait(e, c_wl, free)
                dst = stage if src.dtype == FP32 else stage.bitcast(INT32)
                e.dma_start(dst.rearrange("p (t n) -> p t n", t=src.shape[0] // P),
                            src.rearrange("(t p) n -> p t n", p=P)).then_inc(s_w[w], 16)
            e.wait_ge(s_const, 12)
            run("sp", e)
            e.wait_ge(s_out, 32 * B)

        @block.scalar
        def _(e):
            for n, (w, src, stage, _) in enumerate(WEIGHTS):
                if src.dtype == FP32:
                    e.wait_ge(s_w[w], 16)
                else:
                    e.wait_ge(c_wf, "gud".index(w) + 1)
                e.activation(r(W[w][0][:]).rearrange("p t n -> p (t n)"), stage, ACT.Copy).then_inc(c_wh, 1)
            e.wait_ge(s_const, 12)
            run("act", e)

        @block.vector
        def _(e):
            for n, (w, src, stage, _) in enumerate(WEIGHTS):
                e.wait_ge(s_w[w], 16)
                if src.dtype != FP32:
                    e.tensor_copy(stage, stage.bitcast(INT32)).then_inc(c_wf, 1)
                e.wait_ge(c_wh, n + 1)
                e.tensor_tensor(r(W[w][1][:]).rearrange("p t n -> p (t n)"), stage,
                                W[w][0][:].rearrange("p t n -> p (t n)"), ALU.subtract).then_inc(c_wl, 1)
            run("dve", e)

        @block.tensor
        def _(e):
            e.wait_ge(s_const, 12)
            nc.tensor.matmul(PVB[:], ZERO[:, 0:P], ZERO[:], start=True, stop=True).then_inc(s_fixed, 1)
            e.wait_ge(c_wl, len(W))
            run("pe", e)


_IN = [("x", "L0_attn_x"), ("wqT", "L0_attn_Wq"), ("wkT", "L0_attn_Wk"), ("wvT", "L0_attn_Wv"), ("woT", "L0_attn_Wo"),
       ("wgT", "L0_ffn_w_gate"), ("wuT", "L0_ffn_w_up"), ("wdT", "L0_ffn_w_down")]


def kernel(**inputs):
    import numpy as np
    import concourse.bacc as bacc
    from concourse.bass_utils import run_bass_kernel_spmd

    nc = bacc.Bacc("TRN2", target_bir_lowering=False, num_devices=1, dynamic_dma_scratch_size=1024)
    arrays, args = {}, []
    for name, source in _IN:
        a = np.asarray(inputs[source])
        a = np.ascontiguousarray(a if name == "x" else a.T)
        arrays[name] = a
        args.append(nc.dram_tensor(name, a.shape, mybir.dt.from_np(a.dtype), kind="ExternalInput").ap())
    out = nc.dram_tensor("out", [B, S, E], FP32, kind="ExternalOutput").ap()
    scratch_qk = nc.dram_tensor("scratch_qk", [2, 2, E, S], FP32).ap()
    scratch_o = nc.dram_tensor("scratch_o", [H * 32, S], FP32).ap()
    build(nc, *args, out, scratch_qk, scratch_o)
    r = run_bass_kernel_spmd(nc, [arrays], core_ids=[0])
    return r.results[0]["out"]
```

```python
import concourse.bass as bass
from concourse import mybir
from contextlib import ExitStack

FP32, F32R, BF16, INT32 = mybir.dt.float32, mybir.dt.float32r, mybir.dt.bfloat16, mybir.dt.int32
ACT = mybir.ActivationFunctionType
ALU = mybir.AluOpType
AX = mybir.AxisListType

P = 128
B, S, E = 16, 512, 256
LOOPS = (B - 3) // 2
H = 16
D = E // H
F = 768
KT = E // P
FT = F // P
TT = S // P
PAIRS = H // 2
HALF = 2 * P
ROWS = 3 * D
MROW = ROWS
VW = D + 1
SCALE_W = 1.0 / 127.0
SCALE_S = 1.0 / D ** 0.5
EPS = 1e-5
MASKED = -3.0e38
SEG = [(0,), (1,), (2, 3)]

COUNT = dict(
    f_tr=KT, f_qk=4, f_v=2, f_gu=2 * FT, f_dn=TT, f_op=TT, f_mt=1, f_sm=44, f_st=48, f_pv=12,
    d_ln=3, d_rs=1, d_rc=2, d_xn=1, d_xh=KT, d_xl=KT, d_qh=4, d_ql=4, d_v=2, d_t=2 * FT, d_a=2 * FT, d_h=2 * FT,
    d_hh=2 * FT, d_hl=2 * FT, d_t2=TT, d_g=TT, d_y=TT, d_fin=TT, d_nmh=1, d_nml=1, d_sm=44, d_ex=48,
    d_mk=12, d_ov=4, d_on=2, d_oh=2, d_ol=2)


def maxima_banks():
    banks = []
    for first in (0, PAIRS // 2):
        for parity in (0, 1):
            for i, together in ((0, 4), (1, 2), (2, 1), (3, 1)):
                for j in range(first, first + PAIRS // 2, together):
                    banks.append((i, parity, range(j, j + together)))
    return banks


MAXIMA = maxima_banks()


def merge(a, b):
    out, ta, tb = [], sum(c for c, _ in a), sum(c for c, _ in b)
    i = j = 0
    ca = cb = 0.0
    while i < len(a) or j < len(b):
        if j >= len(b) or (i < len(a) and ca / ta <= cb / tb):
            ca += a[i][0]
            out.append(a[i])
            i += 1
        else:
            cb += b[j][0]
            out.append(b[j])
            j += 1
    return out


def attention_units():
    units = []
    for n in range(13):
        if n < 12:
            for c in range(4):
                units.append(((.22, .16, .22)[n % 3], ("st", 0, 4 * n + c)))
        if n:
            units.append(((1.0, .8, 1.0)[(n - 1) % 3], ("pv", 0, n - 1)))
        if n in (6, 7, 8, 10):
            units.append((0., ({6: "od", 7: "or", 8: "ob", 10: "on"}[n], 0, 0)))
    return units


def gated(ahead, first, last):
    units = []
    for k in range(first, last):
        units.append((1.3, ("gu", ahead, k)))
        if k > 0:
            units.append((0., ("hs", ahead, k - 1)))
    return units


PAUSE = [(4.0, None)]


def schedule(parity, last=True, current=True, following=True, after_next=True):
    def one(kind, ahead, k, cost=0.):
        return [(cost, (kind, ahead, k))]

    head = one("od", -1, 1) + gated(0, 9, 10) + one("lb", 1, 0) + gated(0, 10, 12) + one("or", -1, 1)
    fill = one("tr", 1, 0, .5) + one("tr", 1, 1, .5) + one("hs", 0, 11) + one("ob", -1, 1) + PAUSE + one("dn", 0, 2, 2.)
    fill += [u for k in range(4) for u in one("qk", 1, k, 1.3)] + one("on", -1, 1)
    fill += one("ls", 1, 0) + one("ls", 1, 1) + one("dn", 0, 3, 2.) + one("v", 1, 0, 1.3) + one("v", 1, 1, 1.3)
    fill += [u for j in range(TT) for u in one("op", -1, j, .7)] + gated(1, 0, 2) + one("xc", 1, 0)
    maxima = [(.4, ("sm", 1, k)) for k in range(len(MAXIMA))]
    maxima[20:20] = one("ld", 2, 0)
    ffn = gated(1, 2, 6) + one("hs", 1, 5) + one("gu", 1, 6, 1.3) + one("dn", 1, 0, 2.) + one("dn", 1, 1, 2.) + one("hs", 1, 6)
    fill += merge(maxima, ffn) + one("gu", 1, 7, 1.3) + one("mt", 1, 0) + one("la", 2, 0) + gated(1, 8, 9)
    units, n = [], FIRST_BANK[parity]
    for _, u in head + merge(attention_units(), fill):
        if u is None:
            continue
        bank = None
        if u[0] in RELEASED:
            bank = n % RING
            n += 1
        if {-1: last, 0: current, 1: following, 2: after_next}[u[1]]:
            units.append((*u, bank))
    return units


RELEASED = dict(tr="d_xl", qk="d_ql", v="d_v", gu="d_h", dn="d_g", op="d_y", mt="d_nml", sm="d_sm", st="d_ex")
RING = 7
TURNS = sum(COUNT[f"f_{kind}"] for kind in RELEASED)
FIRST_BANK = (0, TURNS % RING)


def build(nc, x, wqT, wkT, wvT, woT, wgT, wuT, wdT, out, scratch_qk, scratch_o, scratch_r):
    with ExitStack() as ctx:
        def sb(name, shape, dt=FP32):
            return ctx.enter_context(nc.sbuf_tensor(name, shape, dt))

        def bank(name):
            return ctx.enter_context(nc.psum_tensor(name, [P, 512], FP32))

        def sem(name):
            return ctx.enter_context(nc.semaphore(name))

        W = {w: [sb(f"w{w}_{part}", [P, k, n]) for part in ("hi", "lo")]
             for w, k, n in (("k", KT, E), ("q", KT, E), ("v", KT, E), ("g", KT, F), ("u", KT, F), ("d", FT, E), ("o", KT, E))}
        X = [sb(f"x{i}", [P, TT, E]) for i in range(2)]
        XIN = sb("x_in", [P, TT, E])
        XN = sb("xn", [P, TT, E])
        STATS = sb("stats", [P, TT, 6])
        MV = sb("mv", [P, TT, 2])
        VAR = sb("var", [P, TT])
        RSTD = sb("rstd", [P, TT])
        MINUS_HALF = sb("minus_half", [P, TT])
        XT = [sb(f"xt_{part}", [P, KT, S]) for part in ("hi", "lo")]
        QKP = [sb(f"qk_{part}", [P, 2, S]) for part in ("hi", "lo")]
        QS = [sb(f"q_stack{i}", [P, PAIRS, S]) for i in range(2)]
        KS = [sb(f"k_stack{i}", [P, PAIRS, S]) for i in range(2)]
        V = [sb(f"v{i}", [P, TT, H, VW]) for i in range(2)]
        MX = sb("row_max", [P, 64])
        NM = [sb(f"neg_max_{part}", [64, P]) for part in ("hi", "lo")]
        PR = sb("probs", [P, 2, 4, 512])
        O = sb("o", [P, 2, S])
        OC = sb("o_compact", [P, S])
        SUMS = sb("sums", [64, 64])
        RSUMS = sb("sum_reciprocals", [64, 64])
        RDEN = sb("o_reciprocals", [P, S])
        OT = [sb(f"o_{part}", [P, KT, S]) for part in ("hi", "lo")]
        T = sb("tanh", [P, 2, HALF])
        HF = sb("h", [P, 2, HALF])
        HT = [sb(f"h_{part}", [P, FT, HALF]) for part in ("hi", "lo")]
        T2 = sb("tanh_out", [P, E])
        GATES = sb("gates", [P, 2, TT, E])
        G = [GATES[:, i, :, :] for i in range(2)]
        Y = sb("y", [P, 2, E])
        IDF = sb("identity", [P, P])
        IDB = sb("identity_bf16", [P, P], BF16)
        MASK = sb("causal_mask", [P, 4, P], BF16)
        ZERO = sb("zeros", [P, 512], BF16)

        BANKS = [bank(f"bank{i}") for i in range(RING)]
        PVB = bank("values")

        sems = {name: sem(name) for name in COUNT}
        s_const, s_fixed, s_passed = sem("s_const"), sem("s_fixed"), sem("s_passed")
        s_w = {w: sem(f"s_w{w}") for w in W}
        c_wf, c_wh, c_wl = sem("c_wf"), sem("c_wh"), sem("c_wl")
        s_xc, s_sum, s_rst = sem("s_xc"), sem("s_sum"), sem("s_rst")
        s_x, s_out, s_m = sem("s_x"), sem("s_out"), sem("s_m")
        s_qkst = [sem(f"s_qkst{i}") for i in range(2)]
        s_stack = {w: sem(f"s_stack_{w}") for w in "kq"}
        s_ost = [sem(f"s_ost{i}") for i in range(2)]
        s_oc = [sem(f"s_oc{i}") for i in range(2)]

        def r(ap):
            return ap.bitcast(F32R)

        def nth(name, beta, k):
            return beta * COUNT[name] + k + 1

        def wait(e, s, value, apart=False):
            if isinstance(value, int) and value <= 0:
                return
            e.wait_ge(s, value)
            if (apart or e is nc.sync) and not isinstance(value, int):
                e.sem_inc(s_passed, 1)

        def after(e, name, beta, k, apart=False):
            wait(e, sems[name], nth(name, beta, k), apart)

        def signal(ins, name):
            ins.then_inc(sems[name], 1)

        def parts_product(dst, lhs, rhs, start, stop):
            todo = [(0, 0), (0, 1), (1, 0)]
            for j, (a, b) in enumerate(todo):
                last = nc.tensor.matmul(dst, r(lhs[a]), r(rhs[b]), start=start and j == 0, stop=stop and j == 2)
            return last

        def u_ld(en, e, beta, par, k, bank, prev):
            if en == "sp":
                after(e, "d_xn", beta - 1, 0)
                wait(e, s_xc, 16 * beta)
                e.dma_start(XIN[:], x[beta].rearrange("(t p) e -> p t e", p=P)).then_inc(s_x, 16)

        def u_xc(en, e, beta, par, k, bank, prev):
            if en == "sp":
                wait(e, s_out, 32 * (beta - 1))
                wait(e, s_x, 16 * (beta + 1))
                e.dma_start(X[par][:], XIN[:]).then_inc(s_xc, 16)

        def u_la(en, e, beta, par, k, bank, prev):
            if en == "dve":
                wait(e, s_x, 16 * (beta + 1))
                for t in range(TT):
                    last = e.bn_stats(STATS[:, t, :], XIN[:, t, :])
                signal(last, "d_ln")
                after(e, "d_ln", beta, 0, apart=True)
                for t in range(TT):
                    last = e.bn_aggr(MV[:, t, :], STATS[:, t, :])
                signal(last, "d_ln")
                after(e, "d_ln", beta, 1)
                signal(e.tensor_scalar_add(VAR[:], MV[:, :, 1], EPS), "d_ln")
            elif en == "pool":
                after(e, "d_ln", beta, 2)
                signal(e.tensor_tensor(RSTD[:], VAR[:], MINUS_HALF[:], ALU.pow), "d_rs")

        def u_lb(en, e, beta, par, k, bank, prev):
            if en == "dve":
                after(e, "d_rs", beta, 0)
                after(e, "f_tr", beta - 1, KT - 1)
                for t in range(TT):
                    last = e.tensor_scalar(XN[:, t, :], XIN[:, t, :], MV[:, t, 0:1], RSTD[:, t:t + 1],
                                           ALU.subtract, ALU.mult)
                signal(last, "d_xn")

        def u_tr(en, e, beta, par, k, bank, prev):
            if en == "pe":
                after(e, "d_xn", beta, 0)
                prev(e)
                for t in range(TT):
                    last = e.transpose(bank[:, t * P:(t + 1) * P], XN[:, t, k * P:(k + 1) * P], IDF[:])
                signal(last, "f_tr")
            elif en == "act":
                after(e, "f_tr", beta, k)
                signal(e.activation(r(XT[0][:, k, :]), bank[:], ACT.Copy), "d_xh")
            elif en == "dve":
                after(e, "d_xh", beta, k)
                signal(e.tensor_tensor(r(XT[1][:, k, :]), bank[:], XT[0][:, k, :], ALU.subtract), "d_xl")

        def u_qk(en, e, beta, par, k, bank, prev):
            w, m = "kkqq"[k], k % 2
            if en == "pe":
                after(e, "d_xl", beta, KT - 1)
                prev(e)
                for t in range(KT):
                    last = parts_product(bank[:], [part[:, t, m * P:(m + 1) * P] for part in W[w]],
                                         [part[:, t, :] for part in XT], t == 0, t == KT - 1)
                signal(last, "f_qk")
            elif en == "act":
                after(e, "f_qk", beta, k)
                wait(e, s_qkst[m], 64 * beta + 32 * (k // 2))
                signal(e.activation(r(QKP[0][:, m, :]), bank[:], ACT.Copy), "d_qh")
            elif en == "dve":
                after(e, "d_qh", beta, k)
                signal(e.tensor_tensor(r(QKP[1][:, m, :]), bank[:], QKP[0][:, m, :], ALU.subtract), "d_ql")
            elif en == "sp":
                wait(e, s_stack[w], 96 * beta)
                after(e, "d_ql", beta, k)
                for part in range(2):
                    e.dma_start(scratch_qk[k // 2, part, m * P:(m + 1) * P, :], QKP[part][:, m, :])\
                     .then_inc(s_qkst[m], 16)

        def u_ls(en, e, beta, par, k, bank, prev):
            if en == "sp":
                for m in range(2):
                    wait(e, s_qkst[m], 64 * beta + 32 * (k + 1))
                stack, order = ((KS[par], (0, 0, 1)), (QS[par], (0, 1, 0)))[k]
                for slot, part in enumerate(order):
                    rows = scratch_qk[k, part].rearrange("(pair parity d) s -> parity d pair s", parity=2, d=D)
                    for parity in range(2):
                        at = 64 * parity + D * slot
                        e.dma_start(stack[at:at + D, :, :], rows[parity]).then_inc(s_stack["kq"[k]], 16)

        def u_v(en, e, beta, par, k, bank, prev):
            if en == "pe":
                prev(e)
                for j in range(2):
                    t = 2 * k + j
                    for kt in range(KT):
                        last = parts_product(bank[:, j * E:(j + 1) * E], [part[:, kt, t * P:(t + 1) * P] for part in XT],
                                             [part[:, kt, :] for part in W["v"]], kt == 0, kt == KT - 1)
                signal(last, "f_v")
            elif en == "act":
                after(e, "f_v", beta, k)
                for j in range(2):
                    last = e.activation(V[par][:, 2 * k + j, :, 0:D],
                                        bank[:, j * E:(j + 1) * E].rearrange("p (h d) -> p h d", d=D), ACT.Copy)
                signal(last, "d_v")

        def u_gu(en, e, beta, par, k, bank, prev):
            half, f = divmod(k, FT)
            slot = k % 2
            if en == "pe":
                prev(e)
                for j, w in enumerate("gu"):
                    for kt in range(KT):
                        last = parts_product(bank[:, j * HALF:(j + 1) * HALF],
                                             [part[:, kt, f * P:(f + 1) * P] for part in W[w]],
                                             [part[:, kt, half * HALF:(half + 1) * HALF] for part in XT],
                                             kt == 0, kt == KT - 1)
                signal(last, "f_gu")
            elif en == "act":
                after(e, "f_gu", beta, k)
                after(e, "d_h", beta, k - 2)
                signal(e.activation(T[:, slot, :], bank[:, 0:HALF], ACT.Tanh, scale=0.5 * SCALE_W), "d_t")
            elif en == "dve":
                after(e, "d_t", beta, k)
                signal(e.scalar_tensor_tensor(out=T[:, slot, :], in0=T[:, slot, :], scalar=1.0, in1=bank[:, 0:HALF],
                                              op0=ALU.add, op1=ALU.mult), "d_a")
                after(e, "d_a", beta, k)
                after(e, "d_hl", beta, k - 2)
                signal(e.scalar_tensor_tensor(out=HF[:, slot, :], in0=bank[:, HALF:2 * HALF],
                                              scalar=0.5 * SCALE_W * SCALE_W, in1=T[:, slot, :],
                                              op0=ALU.mult, op1=ALU.mult), "d_h")

        def u_hs(en, e, beta, par, k, bank, prev):
            f, slot = k % FT, k % 2
            if en == "act":
                if k == FT:
                    after(e, "f_dn", beta, 1)
                after(e, "d_h", beta, k)
                signal(e.activation(r(HT[0][:, f, :]), HF[:, slot, :], ACT.Copy), "d_hh")
            elif en == "pool":
                after(e, "d_hh", beta, k)
                signal(e.tensor_tensor(r(HT[1][:, f, :]), HF[:, slot, :], HT[0][:, f, :], ALU.subtract), "d_hl")

        def u_dn(en, e, beta, par, k, bank, prev):
            half, j = divmod(k, 2)
            if en == "pe":
                after(e, "d_hl", beta, half * FT + FT - 1)
                prev(e)
                for f in range(FT):
                    last = parts_product(bank[:, 0:E], [part[:, f, j * P:(j + 1) * P] for part in HT],
                                         [part[:, f, :] for part in W["d"]], f == 0, f == FT - 1)
                signal(last, "f_dn")
            elif en == "act":
                after(e, "f_dn", beta, k)
                after(e, "d_g", beta, k - 1)
                signal(e.activation(T2[:], bank[:, 0:E], ACT.Tanh, scale=0.5 * SCALE_W), "d_t2")
            elif en == "dve":
                after(e, "d_t2", beta, k)
                signal(e.scalar_tensor_tensor(out=G[par][:, k, :], in0=T2[:], scalar=1.0, in1=bank[:, 0:E],
                                              op0=ALU.add, op1=ALU.mult), "d_g")

        def u_sm(en, e, beta, par, k, bank, prev):
            i, parity, pairs = MAXIMA[k]
            keys, n = P * (i + 1), len(pairs)
            low = 64 * parity
            scores = bank[:, 0:n * keys].rearrange("p (n t) -> p n t", n=n)
            if en == "pe":
                if k == 0:
                    for w in "kq":
                        wait(e, s_stack[w], 96 * (beta + 1))
                prev(e)
                for j, pair in enumerate(pairs):
                    nc.tensor.matmul(scores[:, j, :], r(QS[par][low:low + ROWS, pair, i * P:(i + 1) * P]),
                                     r(KS[par][low:low + ROWS, pair, 0:keys]), start=j == 0, stop=False,
                                     skip_group_check=True)
                last = nc.tensor.matmul(scores[:, :, i * P:keys], IDB[:], MASK[:, 0:n, :], start=False, stop=True,
                                        skip_group_check=True)
                signal(last, "f_sm")
            elif en == "dve":
                after(e, "f_sm", beta, k)
                at = parity * 32 + pairs[0] * 4 + i
                signal(e.tensor_reduce(MX[:, at:at + 4 * (n - 1) + 1:4], scores, axis=AX.X, op=ALU.max), "d_sm")

        def u_mt(en, e, beta, par, k, bank, prev):
            if en == "pe":
                prev(e)
                after(e, "d_sm", beta, len(MAXIMA) - 1, apart=True)
                signal(e.transpose(bank[0:64, 0:P], MX[:], IDF[:]), "f_mt")
            elif en == "act":
                after(e, "f_mt", beta, 0)
                wait(e, s_m, 64 * beta)
                signal(e.activation(r(NM[0][:]), bank[0:64, 0:P], ACT.Copy, scale=-1.0), "d_nmh")
            elif en == "dve":
                after(e, "d_nmh", beta, 0)
                signal(e.scalar_tensor_tensor(out=r(NM[1][:]), in0=bank[0:64, 0:P], scalar=-1.0, in1=NM[0][:],
                                              op0=ALU.mult, op1=ALU.subtract), "d_nml")
            elif en == "sp":
                after(e, "d_nml", beta, 0)
                for parity in range(2):
                    for part in range(2):
                        row = 64 * parity + MROW + part
                        e.dma_start(QS[par][row:row + 1, :, :].rearrange("o a (i s) -> o (a i) s", i=TT),
                                    NM[part][32 * parity:32 * parity + 32, :]).then_inc(s_m, 16)

        def segment_offsets(seg):
            at = 0
            for j in SEG[seg]:
                yield j, at, S - j * P
                at += S - j * P

        def u_st(en, e, beta, par, k, bank, prev):
            g, rest = divmod(k, 12)
            seg, c = divmod(rest, 4)
            n = 3 * g + seg
            head = 4 * g + c
            low, pair = 64 * (head % 2), head // 2
            width = sum(w for _, _, w in segment_offsets(seg))
            if en == "pe":
                if k == 0:
                    wait(e, s_m, 64 * (beta + 1))
                prev(e)
                for j, at, w in segment_offsets(seg):
                    last = nc.tensor.matmul(bank[:, at:at + w], r(KS[par][low:low + ROWS + 2, pair, j * P:(j + 1) * P]),
                                            r(QS[par][low:low + ROWS + 2, pair, j * P:S]), start=True, stop=True)
                signal(last, "f_st")
            elif en == "act":
                if c == 0:
                    after(e, "f_pv", beta, n - 2)
                after(e, "f_st", beta, k)
                signal(e.activation(PR[:, n % 2, c, 0:width], bank[:, 0:width], ACT.Exp, scale=SCALE_S), "d_ex")
            elif en == "pool" and c == 3:
                after(e, "d_ex", beta, k, apart=True)
                tiles = len(SEG[seg])
                diag = PR[:, n % 2, :, :].rearrange("p c (b s) -> p c b s", s=HALF)[:, :, 0:tiles, 0:P]
                signal(e.affine_select(out=diag, in_=diag, compare_op=ALU.is_ge, fill=0.0, base=0,
                                       pattern=[[0, 4], [0, tiles], [1, P]], channel_multiplier=-1), "d_mk")

        def u_pv(en, e, beta, par, k, bank, prev):
            g, seg = divmod(k, 3)
            if en == "pe":
                if k == 0:
                    after(e, "d_v", beta, 1)
                if seg == 0:
                    after(e, "d_ov", beta, g - 1)
                after(e, "d_mk", beta, k)
                for j, at, w in segment_offsets(seg):
                    for c in range(4):
                        last = nc.tensor.matmul(PVB[32 * c:32 * c + VW, j * P:S], V[par][:, j, 4 * g + c, :],
                                                PR[:, k % 2, c, at:at + w], start=j == 0, stop=j == TT - 1)
                signal(last, "f_pv")
            elif en == "act" and seg == 2:
                wait(e, s_ost[g % 2], 32 * beta + 16 * (g // 2))
                after(e, "f_pv", beta, k)
                signal(e.activation(O[:, g % 2, :], PVB[:], ACT.Copy), "d_ov")
            elif en == "sp" and seg == 2:
                wait(e, s_oc[g // 2], 32 * beta)
                after(e, "d_ov", beta, g)
                e.dma_start(scratch_o[g * P:(g + 1) * P, :], O[:, g % 2, :]).then_inc(s_ost[g % 2], 16)

        def heads8(k):
            return scratch_o[k * 2 * P:(k + 1) * 2 * P, :].rearrange("(h r) s -> h r s", r=32)

        def u_od(en, e, beta, par, k, bank, prev):
            if en == "sp":
                for m in range(2):
                    wait(e, s_ost[m], 32 * beta + 16 * (k + 1))
                after(e, "d_ol", beta, k - 1)
                e.dma_start(SUMS[:], heads8(k)[:, D, :].rearrange("h (a s) -> h a s", s=64)).then_inc(s_sum, 16)
                e.dma_start(OC[:], heads8(k)[:, 0:D, :]).then_inc(s_oc[k], 16)

        def u_or(en, e, beta, par, k, bank, prev):
            if en == "dve":
                wait(e, s_sum, 32 * beta + 16 * (k + 1))
                signal(e.reciprocal(RSUMS[:], SUMS[:]), "d_rc")
            elif en == "sp":
                after(e, "d_rc", beta, k)
                e.dma_start(scratch_r[k].rearrange("h (a s) -> (h a) s", s=64), RSUMS[:]).then_inc(s_rst, 16)

        def u_ob(en, e, beta, par, k, bank, prev):
            if en == "sp":
                wait(e, s_rst, 32 * beta + 16 * (k + 1))
                e.dma_start(RDEN[:], scratch_r[k].rearrange("h (o s) -> h o s", o=1).to_broadcast([8, D, S])).then_inc(s_oc[k], 16)

        def u_on(en, e, beta, par, k, bank, prev):
            if en == "pool":
                wait(e, s_oc[k], 32 * (beta + 1))
                signal(e.tensor_tensor(OC[:], OC[:], RDEN[:], ALU.mult), "d_on")
            elif en == "act":
                after(e, "d_on", beta, k)
                signal(e.activation(r(OT[0][:, k, :]), OC[:], ACT.Copy), "d_oh")
            elif en == "dve":
                after(e, "d_oh", beta, k)
                signal(e.tensor_tensor(r(OT[1][:, k, :]), OC[:], OT[0][:, k, :], ALU.subtract), "d_ol")

        def u_op(en, e, beta, par, k, bank, prev):
            if en == "pe":
                after(e, "d_ol", beta, 1)
                prev(e)
                for kt in range(KT):
                    last = parts_product(bank[:, 0:E], [part[:, kt, k * P:(k + 1) * P] for part in OT],
                                         [part[:, kt, :] for part in W["o"]], kt == 0, kt == KT - 1)
                signal(last, "f_op")
            elif en == "dve":
                after(e, "f_op", beta, k)
                after(e, "d_fin", beta, max(k - 2, -1))
                signal(e.scalar_tensor_tensor(out=Y[:, k % 2, :], in0=bank[:, 0:E], scalar=0.5 * SCALE_W, in1=G[par][:, k, :],
                                              op0=ALU.mult, op1=ALU.mult), "d_y")
            elif en == "pool":
                after(e, "d_y", beta, k)
                if k == 0:
                    wait(e, s_xc, 16 * (beta + 1))
                signal(e.tensor_tensor(X[par][:, k, :], Y[:, k % 2, :], X[par][:, k, :], ALU.add), "d_fin")
            elif en == "sp" and k % 2:
                after(e, "d_fin", beta, k)
                e.dma_start(out[beta].rearrange("(t p) e -> p t e", p=P)[:, k - 1:k + 1, :],
                            X[par][:, k - 1:k + 1, :]).then_inc(s_out, 16)

        UNIT = dict(ld=u_ld, la=u_la, lb=u_lb, tr=u_tr, qk=u_qk, ls=u_ls, v=u_v, gu=u_gu, hs=u_hs, dn=u_dn, sm=u_sm,
                    mt=u_mt, st=u_st, pv=u_pv, od=u_od, ob=u_ob, on=u_on, op=u_op, xc=u_xc)
        UNIT["or"] = u_or

        def step(en, e, b, parity, units, users):
            for kind, ahead, k, n in units:
                def prev(e, n=n):
                    if n in users:
                        last, last_ahead, last_k = users[n]
                        after(e, RELEASED[last], b + last_ahead, last_k)
                UNIT[kind](en, e, b + ahead, (parity + ahead) % 2, k, None if n is None else BANKS[n], prev)
                if n is not None:
                    users[n] = (kind, ahead, k)
            return {n: (kind, ahead - 1, k) for n, (kind, ahead, k) in users.items()}

        def run(en, e):
            if en in ("sp", "dve", "pool"):
                for kind in ("ld", "la"):
                    UNIT[kind](en, e, 0, 0, 0, None, None)
            users = step(en, e, -1, 1, schedule(1, last=False, current=False), {})
            if en in ("act", "sp"):
                wait(e, c_wl, len(W))
            users = step(en, e, 0, 0, schedule(0, last=False), users)
            with e.Fori(0, LOOPS) as pair:
                b = 2 * pair + 1
                after_one = step(en, e, b, 1, schedule(1), dict(users))
                step(en, e, b + 1, 0, schedule(0), after_one)
            for b in range(2 * LOOPS + 1, B + 1):
                ends = schedule(b % 2, current=b < B, following=b + 1 < B, after_next=b + 2 < B)
                users = step(en, e, b, b % 2, ends, users)

        stage_p = PR[:].rearrange("p a b c -> p (a b c)")
        stage_g = GATES[:].rearrange("p a t e -> p (a t e)")
        WEIGHTS = [
            ("k", wkT, stage_p[:, 0:512], 0), ("q", wqT, stage_p[:, 512:1024], 0), ("v", wvT, stage_p[:, 1024:1536], 0),
            ("g", wgT, stage_p[:, 1536:3072], 0), ("u", wuT, stage_g[:, 0:1536], 0),
            ("o", woT, stage_p[:, 3072:3584], 0), ("d", wdT, stage_p[:, 0:1536], 3)]

        block = ctx.enter_context(nc.Block())

        @block.gpsimd
        def _(e):
            e.memset(IDF[:], 0.0).then_inc(s_const, 1)
            e.memset(IDB[:], 0.0).then_inc(s_const, 1)
            e.memset(MASK[:], 0.0).then_inc(s_const, 1)
            e.memset(ZERO[:], 0.0).then_inc(s_const, 1)
            e.memset(MINUS_HALF[:], -0.5).then_inc(s_const, 1)
            e.wait_ge(s_const, 5)
            for m in (IDF, IDB):
                e.affine_select(out=m[:], in_=m[:], compare_op=ALU.not_equal, fill=1.0, base=0,
                                pattern=[[-1, P]], channel_multiplier=1).then_inc(s_const, 1)
            e.affine_select(out=MASK[:], in_=MASK[:], compare_op=ALU.is_ge, fill=MASKED, base=0,
                            pattern=[[0, 4], [-1, P]], channel_multiplier=1).then_inc(s_const, 1)
            for stack in KS:
                e.memset(stack[:], 1.0).then_inc(s_const, 1)
            for v in V:
                e.memset(v[:], 1.0).then_inc(s_const, 1)
            run("pool", e)

        @block.sync
        def _(e):
            for w, src, stage, free in WEIGHTS:
                wait(e, c_wl, free)
                dst = stage if src.dtype == FP32 else stage.bitcast(INT32)
                e.dma_start(dst.rearrange("p (t n) -> p t n", t=src.shape[0] // P),
                            src.rearrange("(t p) n -> p t n", p=P)).then_inc(s_w[w], 16)
            e.wait_ge(s_const, 12)
            run("sp", e)
            e.wait_ge(s_out, 32 * B)

        @block.scalar
        def _(e):
            for n, (w, src, stage, _) in enumerate(WEIGHTS):
                if src.dtype == FP32:
                    e.wait_ge(s_w[w], 16)
                else:
                    e.wait_ge(c_wf, "gud".index(w) + 1)
                e.activation(r(W[w][0][:]).rearrange("p t n -> p (t n)"), stage, ACT.Copy).then_inc(c_wh, 1)
            e.wait_ge(s_const, 12)
            run("act", e)

        @block.vector
        def _(e):
            for n, (w, src, stage, _) in enumerate(WEIGHTS):
                e.wait_ge(s_w[w], 16)
                if src.dtype != FP32:
                    e.tensor_copy(stage, stage.bitcast(INT32)).then_inc(c_wf, 1)
                e.wait_ge(c_wh, n + 1)
                e.tensor_tensor(r(W[w][1][:]).rearrange("p t n -> p (t n)"), stage,
                                W[w][0][:].rearrange("p t n -> p (t n)"), ALU.subtract).then_inc(c_wl, 1)
            run("dve", e)

        @block.tensor
        def _(e):
            e.wait_ge(s_const, 12)
            nc.tensor.matmul(PVB[:], ZERO[:, 0:P], ZERO[:], start=True, stop=True).then_inc(s_fixed, 1)
            e.wait_ge(c_wl, len(W))
            run("pe", e)


_IN = [("x", "L0_attn_x"), ("wqT", "L0_attn_Wq"), ("wkT", "L0_attn_Wk"), ("wvT", "L0_attn_Wv"), ("woT", "L0_attn_Wo"),
       ("wgT", "L0_ffn_w_gate"), ("wuT", "L0_ffn_w_up"), ("wdT", "L0_ffn_w_down")]


def kernel(**inputs):
    import numpy as np
    import concourse.bacc as bacc
    from concourse.bass_utils import run_bass_kernel_spmd

    nc = bacc.Bacc("TRN2", target_bir_lowering=False, num_devices=1, dynamic_dma_scratch_size=1024)
    arrays, args = {}, []
    for name, source in _IN:
        a = np.asarray(inputs[source])
        a = np.ascontiguousarray(a if name == "x" else a.T)
        arrays[name] = a
        args.append(nc.dram_tensor(name, a.shape, mybir.dt.from_np(a.dtype), kind="ExternalInput").ap())
    out = nc.dram_tensor("out", [B, S, E], FP32, kind="ExternalOutput").ap()
    scratch_qk = nc.dram_tensor("scratch_qk", [2, 2, E, S], FP32).ap()
    scratch_o = nc.dram_tensor("scratch_o", [H * 32, S], FP32).ap()
    scratch_r = nc.dram_tensor("scratch_r", [KT, 8, S], FP32).ap()
    build(nc, *args, out, scratch_qk, scratch_o, scratch_r)
    r = run_bass_kernel_spmd(nc, [arrays], core_ids=[0])
    return r.results[0]["out"]
```

```python
import concourse.bass as bass
from concourse import mybir
from contextlib import ExitStack

FP32, F32R, BF16, INT32 = mybir.dt.float32, mybir.dt.float32r, mybir.dt.bfloat16, mybir.dt.int32
ACT = mybir.ActivationFunctionType
ALU = mybir.AluOpType
AX = mybir.AxisListType

P = 128
B, S, E = 16, 512, 256
LOOPS = (B - 3) // 2
H = 16
D = E // H
F = 768
KT = E // P
FT = F // P
TT = S // P
PAIRS = H // 2
HALF = 2 * P
STACK = 64
MROW = STACK - 2
VW = D + 1
SCALE_W = 1.0 / 127.0
SCALE_S = 1.0 / D ** 0.5
EPS = 1e-5
MASKED = -3.0e38
SEG = [(0,), (1,), (2, 3)]

COUNT = dict(
    f_tr=KT, f_qk=4, f_v=2, f_gu=2 * FT, f_dn=TT, f_op=TT, f_mt=1, f_sm=44, f_st=48, f_pv=12,
    d_ln=3, d_rs=1, d_rc=2, d_xn=1, d_xh=KT, d_xl=KT, d_qh=4, d_ql=4, d_v=2, d_t=2 * FT, d_a=2 * FT, d_h=2 * FT,
    d_hh=2 * FT, d_hl=2 * FT, d_t2=TT, d_g=TT, d_y=TT, d_fin=TT, d_nmh=1, d_nml=1, d_sm=44, d_ex=48,
    d_mk=12, d_ov=4, d_on=2, d_oh=2, d_ol=2)


def maxima_banks():
    banks = []
    for first in (0, PAIRS // 2):
        for parity in (0, 1):
            for i, together in ((0, 4), (1, 2), (2, 1), (3, 1)):
                for j in range(first, first + PAIRS // 2, together):
                    banks.append((i, parity, range(j, j + together)))
    return banks


MAXIMA = maxima_banks()


def merge(a, b):
    out, ta, tb = [], sum(c for c, _ in a), sum(c for c, _ in b)
    i = j = 0
    ca = cb = 0.0
    while i < len(a) or j < len(b):
        if j >= len(b) or (i < len(a) and ca / ta <= cb / tb):
            ca += a[i][0]
            out.append(a[i])
            i += 1
        else:
            cb += b[j][0]
            out.append(b[j])
            j += 1
    return out


SOFTMAX_ENDS = {6: "od", 8: "or", 9: "ob", 10: "on", 11: "os"}


def attention_units():
    units = []
    for n in range(13):
        if n < 12:
            for c in range(4):
                units.append(((.22, .16, .22)[n % 3], ("st", 0, 4 * n + c)))
        if n:
            units.append(((1.0, .8, 1.0)[(n - 1) % 3], ("pv", 0, n - 1)))
        if n in SOFTMAX_ENDS:
            units.append((0., (SOFTMAX_ENDS[n], 0, 0)))
    return units


def gated(ahead, first, last):
    units = []
    for k in range(first, last):
        units.append((.9, ("gu", ahead, k)))
        if k > 0:
            units.append((0., ("hs", ahead, k - 1)))
    return units


TAIL = 7


def schedule(parity, last=True, current=True, following=True, after_next=True):
    def one(kind, ahead, k, cost=0.):
        return [(cost, (kind, ahead, k))]

    attention = attention_units()
    tail = [(cost, (kind, -1, k)) for cost, (kind, _, k) in attention[-TAIL:]]
    head = one("lb", 1, 0) + merge(tail[:4], gated(0, 9, 12)) + one("tr", 1, 0) + one("tr", 1, 1)
    head += one("hs", 0, 11) + tail[4:] + one("od", -1, 1)
    fill = one("dn", 0, 2, 1.4) + one("or", -1, 1)
    fill += one("qk", 1, 0, 1.3) + one("ob", -1, 1) + one("qk", 1, 1, 1.3) + one("ls", 1, 0) + one("dn", 0, 3, 1.4)
    fill += one("on", -1, 1) + one("qk", 1, 2, 1.3) + one("os", -1, 1) + one("qk", 1, 3, 1.3) + one("ls", 1, 1)
    fill += one("v", 1, 0, 1.3) + one("v", 1, 1, 1.3)
    fill += [u for j in range(TT) for u in one("op", -1, j, .7)] + gated(1, 0, 2) + one("xc", 1, 0)
    maxima = [(.4, ("sm", 1, k)) for k in range(len(MAXIMA))]
    maxima[4:4] = one("ld", 2, 0)
    ffn = gated(1, 2, 6) + one("hs", 1, 5) + one("gu", 1, 6, .9) + one("dn", 1, 0, 1.4) + one("dn", 1, 1, 1.4) + one("hs", 1, 6)
    fill += merge(maxima, ffn) + one("la", 2, 0) + one("gu", 1, 7, .9) + one("mt", 1, 0) + gated(1, 8, 9)
    units, n = [], FIRST_BANK[parity]
    for _, u in head + merge(attention[:-TAIL], fill):
        bank = None
        if u[0] in RELEASED:
            bank = n % RING
            n += 1
        if {-1: last, 0: current, 1: following, 2: after_next}[u[1]]:
            units.append((*u, bank))
    return units


RELEASED = dict(tr="d_xl", qk="d_ql", v="d_v", gu="d_h", dn="d_g", op="d_y", mt="d_nml", sm="d_sm", st="d_ex")
RING = 7
TURNS = sum(COUNT[f"f_{kind}"] for kind in RELEASED)
FIRST_BANK = (0, TURNS % RING)


def build(nc, x, wqT, wkT, wvT, woT, wgT, wuT, wdT, out, scratch_qk, scratch_o, scratch_r):
    with ExitStack() as ctx:
        def sb(name, shape, dt=FP32):
            return ctx.enter_context(nc.sbuf_tensor(name, shape, dt))

        def bank(name):
            return ctx.enter_context(nc.psum_tensor(name, [P, 512], FP32))

        def sem(name):
            return ctx.enter_context(nc.semaphore(name))

        W = {w: [sb(f"w{w}_{part}", [P, k, n]) for part in ("hi", "lo")]
             for w, k, n in (("k", KT, E), ("q", KT, E), ("v", KT, E), ("g", KT, F), ("u", KT, F), ("d", FT, E), ("o", KT, E))}
        X = [sb(f"x{i}", [P, TT, E]) for i in range(2)]
        XIN = sb("x_in", [P, TT, E])
        XN = sb("xn", [P, TT, E])
        STATS = sb("stats", [P, TT, 6])
        MV = sb("mv", [P, TT, 2])
        VAR = sb("var", [P, TT])
        RSTD = sb("rstd", [P, TT])
        MINUS_HALF = sb("minus_half", [P, TT])
        XT = [sb(f"xt_{part}", [P, KT, S]) for part in ("hi", "lo")]
        QKP = [sb(f"qk_{part}", [P, 2, S]) for part in ("hi", "lo")]
        QS = [sb(f"q_stack{i}", [P, PAIRS, S]) for i in range(2)]
        KS = [sb(f"k_stack{i}", [P, PAIRS, S]) for i in range(2)]
        V = [sb(f"v{i}", [P, TT, H, VW]) for i in range(2)]
        MX = sb("row_max", [P, 64])
        NM = [sb(f"neg_max_{part}", [64, P]) for part in ("hi", "lo")]
        PR = sb("probs", [P, 2, 4, 512])
        O = sb("o", [P, 2, S])
        OC = sb("o_compact", [P, S])
        SUMS = sb("sums", [64, 64])
        RSUMS = sb("sum_reciprocals", [64, 64])
        RDEN = sb("o_reciprocals", [P, S])
        OT = [sb(f"o_{part}", [P, KT, S]) for part in ("hi", "lo")]
        T = sb("tanh", [P, 2, HALF])
        HF = sb("h", [P, 2, HALF])
        HT = [sb(f"h_{part}", [P, FT, HALF]) for part in ("hi", "lo")]
        T2 = sb("tanh_out", [P, E])
        GATES = sb("gates", [P, 2, TT, E])
        G = [GATES[:, i, :, :] for i in range(2)]
        Y = sb("y", [P, 2, E])
        LOW = sb("low_parts", [P, 4])
        LOW1 = sb("low_parts_all", [1, 1])
        FLAG = sb("low_parts_used", [1, 1], INT32)
        IDF = sb("identity", [P, P])
        IDB = sb("identity_bf16", [P, P], BF16)
        MASK = sb("causal_mask", [P, 4, P], BF16)
        ZERO = sb("zeros", [P, 512], BF16)

        BANKS = [bank(f"bank{i}") for i in range(RING)]
        PVB = bank("values")

        sems = {name: sem(name) for name in COUNT}
        s_flag = sem("s_flag")
        s_const, s_fixed, s_passed = sem("s_const"), sem("s_fixed"), sem("s_passed")
        s_w = {w: sem(f"s_w{w}") for w in W}
        c_wf, c_wh, c_wl = sem("c_wf"), sem("c_wh"), sem("c_wl")
        s_xc, s_sum, s_rst = sem("s_xc"), sem("s_sum"), sem("s_rst")
        s_x, s_out, s_m = sem("s_x"), sem("s_out"), sem("s_m")
        s_qkst = [sem(f"s_qkst{i}") for i in range(2)]
        s_stack = [sem(f"s_stack{i}") for i in range(2)]
        s_ost = [sem(f"s_ost{i}") for i in range(2)]
        s_oc = [sem(f"s_oc{i}") for i in range(2)]

        def r(ap):
            return ap.bitcast(F32R)

        def nth(name, beta, k):
            return beta * COUNT[name] + k + 1

        def wait(e, s, value, apart=False):
            if isinstance(value, int) and value <= 0:
                return
            e.wait_ge(s, value)
            if (apart or e is nc.sync) and not isinstance(value, int):
                e.sem_inc(s_passed, 1)

        def after(e, name, beta, k, apart=False):
            wait(e, sems[name], nth(name, beta, k), apart)

        def signal(ins, name):
            ins.then_inc(sems[name], 1)

        def parts_product(dst, lhs, rhs, start, stop, parts=((0, 0), (0, 1), (1, 0))):
            for j, (a, b) in enumerate(parts):
                last = nc.tensor.matmul(dst, r(lhs[a]), r(rhs[b]), start=start and j == 0,
                                        stop=stop and j == len(parts) - 1)
            return last

        def weights_split(e, beta, w):
            if isinstance(beta, int) and beta == 0:
                wait(e, c_wl, ORDER.index(w) + 1)

        short = [False]

        def u_ld(en, e, beta, par, k, bank, prev):
            if en == "sp":
                after(e, "d_xn", beta - 1, 0)
                wait(e, s_xc, 16 * beta)
                e.dma_start(XIN[:], x[beta].rearrange("(t p) e -> p t e", p=P)).then_inc(s_x, 16)

        def u_xc(en, e, beta, par, k, bank, prev):
            if en == "sp":
                wait(e, s_out, 32 * (beta - 1))
                wait(e, s_x, 16 * (beta + 1))
                e.dma_start(X[par][:], XIN[:]).then_inc(s_xc, 16)

        def u_la(en, e, beta, par, k, bank, prev):
            if en == "dve":
                wait(e, s_x, 16 * (beta + 1))
                for t in range(TT):
                    last = e.bn_stats(STATS[:, t, :], XIN[:, t, :])
                signal(last, "d_ln")
                after(e, "d_ln", beta, 0, apart=True)
                for t in range(TT):
                    last = e.bn_aggr(MV[:, t, :], STATS[:, t, :])
                signal(last, "d_ln")
                after(e, "d_ln", beta, 1)
                signal(e.tensor_scalar_add(VAR[:], MV[:, :, 1], EPS), "d_ln")
            elif en == "pool":
                after(e, "d_ln", beta, 2)
                signal(e.tensor_tensor(RSTD[:], VAR[:], MINUS_HALF[:], ALU.pow), "d_rs")

        def u_lb(en, e, beta, par, k, bank, prev):
            if en == "dve":
                after(e, "d_rs", beta, 0)
                after(e, "f_tr", beta - 1, KT - 1)
                for t in range(TT):
                    last = e.tensor_scalar(XN[:, t, :], XIN[:, t, :], MV[:, t, 0:1], RSTD[:, t:t + 1],
                                           ALU.subtract, ALU.mult)
                signal(last, "d_xn")

        def u_tr(en, e, beta, par, k, bank, prev):
            if en == "pe":
                after(e, "d_xn", beta, 0)
                prev(e)
                for t in range(TT):
                    last = e.transpose(bank[:, t * P:(t + 1) * P], XN[:, t, k * P:(k + 1) * P], IDF[:])
                signal(last, "f_tr")
            elif en == "act":
                after(e, "f_tr", beta, k)
                signal(e.activation(r(XT[0][:, k, :]), bank[:], ACT.Copy), "d_xh")
            elif en == "dve":
                after(e, "d_xh", beta, k)
                signal(e.tensor_tensor(r(XT[1][:, k, :]), bank[:], XT[0][:, k, :], ALU.subtract), "d_xl")

        def u_qk(en, e, beta, par, k, bank, prev):
            w, m, slot = "kqkq"[k], k // 2, k % 2
            if en == "pe":
                after(e, "d_xl", beta, KT - 1)
                weights_split(e, beta, w)
                prev(e)
                for t in range(KT):
                    last = parts_product(bank[:], [part[:, t, m * P:(m + 1) * P] for part in W[w]],
                                         [part[:, t, :] for part in XT], t == 0, t == KT - 1)
                signal(last, "f_qk")
            elif en == "act":
                after(e, "f_qk", beta, k)
                wait(e, s_qkst[slot], 64 * beta + 32 * m)
                signal(e.activation(r(QKP[0][:, slot, :]), bank[:], ACT.Copy), "d_qh")
            elif en == "dve":
                after(e, "d_qh", beta, k)
                signal(e.tensor_tensor(r(QKP[1][:, slot, :]), bank[:], QKP[0][:, slot, :], ALU.subtract), "d_ql")
            elif en == "sp":
                wait(e, s_stack[m], 192 * beta)
                after(e, "d_ql", beta, k)
                for part in range(2):
                    e.dma_start(scratch_qk[slot, part, m * P:(m + 1) * P, :], QKP[part][:, slot, :])\
                     .then_inc(s_qkst[slot], 16)

        def u_ls(en, e, beta, par, k, bank, prev):
            if en == "sp":
                for slot in range(2):
                    wait(e, s_qkst[slot], 64 * beta + 32 * (k + 1))
                half = slice(k * PAIRS // 2, (k + 1) * PAIRS // 2)
                for which, stack, order in ((0, KS[par], (0, 0, 1)), (1, QS[par], (0, 1, 0))):
                    for slot, part in enumerate(order):
                        rows = scratch_qk[which, part].rearrange("(pair parity d) s -> parity d pair s", parity=2, d=D)
                        for parity in range(2):
                            at = 64 * parity + D * slot
                            e.dma_start(stack[at:at + D, half, :], rows[parity][:, half, :]).then_inc(s_stack[k], 16)

        def u_v(en, e, beta, par, k, bank, prev):
            if en == "pe":
                weights_split(e, beta, "v")
                prev(e)
                for j in range(2):
                    t = 2 * k + j
                    for kt in range(KT):
                        last = parts_product(bank[:, j * E:(j + 1) * E], [part[:, kt, t * P:(t + 1) * P] for part in XT],
                                             [part[:, kt, :] for part in W["v"]], kt == 0, kt == KT - 1)
                signal(last, "f_v")
            elif en == "act":
                after(e, "f_v", beta, k)
                for j in range(2):
                    last = e.activation(V[par][:, 2 * k + j, :, 0:D],
                                        bank[:, j * E:(j + 1) * E].rearrange("p (h d) -> p h d", d=D), ACT.Copy)
                signal(last, "d_v")

        def u_gu(en, e, beta, par, k, bank, prev):
            half, f = divmod(k, FT)
            slot = k % 2
            if en == "pe":
                weights_split(e, beta, "u")
                prev(e)
                for j, w in enumerate("gu"):
                    for kt in range(KT):
                        last = parts_product(bank[:, j * HALF:(j + 1) * HALF],
                                             [part[:, kt, f * P:(f + 1) * P] for part in W[w]],
                                             [part[:, kt, half * HALF:(half + 1) * HALF] for part in XT],
                                             kt == 0, kt == KT - 1, ((0, 0), (0, 1), (1, 0))[:2 if short[0] else 3])
                signal(last, "f_gu")
            elif en == "act":
                after(e, "f_gu", beta, k)
                after(e, "d_h", beta, k - 2)
                signal(e.activation(T[:, slot, :], bank[:, 0:HALF], ACT.Tanh, scale=0.5 * SCALE_W), "d_t")
            elif en == "dve":
                after(e, "d_t", beta, k)
                signal(e.scalar_tensor_tensor(out=T[:, slot, :], in0=T[:, slot, :], scalar=1.0, in1=bank[:, 0:HALF],
                                              op0=ALU.add, op1=ALU.mult), "d_a")
                after(e, "d_a", beta, k)
                after(e, "d_hl", beta, k - 2)
                signal(e.scalar_tensor_tensor(out=HF[:, slot, :], in0=bank[:, HALF:2 * HALF],
                                              scalar=0.5 * SCALE_W * SCALE_W, in1=T[:, slot, :],
                                              op0=ALU.mult, op1=ALU.mult), "d_h")

        def u_hs(en, e, beta, par, k, bank, prev):
            f, slot = k % FT, k % 2
            if en == "act":
                if k == FT:
                    after(e, "f_dn", beta, 1)
                after(e, "d_h", beta, k)
                signal(e.activation(r(HT[0][:, f, :]), HF[:, slot, :], ACT.Copy), "d_hh")
            elif en == "pool":
                after(e, "d_hh", beta, k)
                signal(e.tensor_tensor(r(HT[1][:, f, :]), HF[:, slot, :], HT[0][:, f, :], ALU.subtract), "d_hl")

        def u_dn(en, e, beta, par, k, bank, prev):
            half, j = divmod(k, 2)
            if en == "pe":
                after(e, "d_hl", beta, half * FT + FT - 1)
                weights_split(e, beta, "d")
                prev(e)
                for f in range(FT):
                    last = parts_product(bank[:, 0:E], [part[:, f, j * P:(j + 1) * P] for part in HT],
                                         [part[:, f, :] for part in W["d"]], f == 0, f == FT - 1,
                                         ((0, 0), (1, 0), (0, 1))[:2 if short[0] else 3])
                signal(last, "f_dn")
            elif en == "act":
                after(e, "f_dn", beta, k)
                after(e, "d_g", beta, k - 1)
                signal(e.activation(T2[:], bank[:, 0:E], ACT.Tanh, scale=0.5 * SCALE_W), "d_t2")
            elif en == "dve":
                after(e, "d_t2", beta, k)
                signal(e.scalar_tensor_tensor(out=G[par][:, k, :], in0=T2[:], scalar=1.0, in1=bank[:, 0:E],
                                              op0=ALU.add, op1=ALU.mult), "d_g")

        def u_sm(en, e, beta, par, k, bank, prev):
            i, parity, pairs = MAXIMA[k]
            keys, n = P * (i + 1), len(pairs)
            low = 64 * parity
            scores = bank[:, 0:n * keys].rearrange("p (n t) -> p n t", n=n)
            if en == "pe":
                if k % (len(MAXIMA) // 2) == 0:
                    wait(e, s_stack[2 * k // len(MAXIMA)], 192 * (beta + 1))
                prev(e)
                for j, pair in enumerate(pairs):
                    nc.tensor.matmul(scores[:, j, :], r(QS[par][low:low + MROW, pair, i * P:(i + 1) * P]),
                                     r(KS[par][low:low + MROW, pair, 0:keys]), start=j == 0, stop=False,
                                     skip_group_check=True)
                last = nc.tensor.matmul(scores[:, :, i * P:keys], IDB[:], MASK[:, 0:n, :], start=False, stop=True,
                                        skip_group_check=True)
                signal(last, "f_sm")
            elif en == "dve":
                after(e, "f_sm", beta, k)
                at = parity * 32 + pairs[0] * 4 + i
                signal(e.tensor_reduce(MX[:, at:at + 4 * (n - 1) + 1:4], scores, axis=AX.X, op=ALU.max), "d_sm")

        def u_mt(en, e, beta, par, k, bank, prev):
            if en == "pe":
                prev(e)
                after(e, "d_sm", beta, len(MAXIMA) - 1, apart=True)
                signal(e.transpose(bank[0:64, 0:P], MX[:], IDF[:]), "f_mt")
            elif en == "act":
                after(e, "f_mt", beta, 0)
                wait(e, s_m, 64 * beta)
                signal(e.activation(r(NM[0][:]), bank[0:64, 0:P], ACT.Copy, scale=-1.0), "d_nmh")
            elif en == "dve":
                after(e, "d_nmh", beta, 0)
                signal(e.scalar_tensor_tensor(out=r(NM[1][:]), in0=bank[0:64, 0:P], scalar=-1.0, in1=NM[0][:],
                                              op0=ALU.mult, op1=ALU.subtract), "d_nml")
            elif en == "sp":
                after(e, "d_nml", beta, 0)
                for parity in range(2):
                    for part in range(2):
                        row = 64 * parity + MROW + part
                        e.dma_start(QS[par][row:row + 1, :, :].rearrange("o a (i s) -> o (a i) s", i=TT),
                                    NM[part][32 * parity:32 * parity + 32, :]).then_inc(s_m, 16)

        def segment_offsets(seg):
            at = 0
            for j in SEG[seg]:
                yield j, at, S - j * P
                at += S - j * P

        def u_st(en, e, beta, par, k, bank, prev):
            g, rest = divmod(k, 12)
            seg, c = divmod(rest, 4)
            n = 3 * g + seg
            head = 4 * g + c
            low, pair = 64 * (head % 2), head // 2
            width = sum(w for _, _, w in segment_offsets(seg))
            if en == "pe":
                if k == 0:
                    wait(e, s_m, 64 * (beta + 1))
                prev(e)
                for j, at, w in segment_offsets(seg):
                    last = nc.tensor.matmul(bank[:, at:at + w], r(KS[par][low:low + STACK, pair, j * P:(j + 1) * P]),
                                            r(QS[par][low:low + STACK, pair, j * P:S]), start=True, stop=True)
                signal(last, "f_st")
            elif en == "act":
                if c == 0:
                    after(e, "f_pv", beta, n - 2)
                after(e, "f_st", beta, k)
                signal(e.activation(PR[:, n % 2, c, 0:width], bank[:, 0:width], ACT.Exp, scale=SCALE_S), "d_ex")
            elif en == "pool" and c == 3:
                after(e, "d_ex", beta, k, apart=True)
                tiles = len(SEG[seg])
                diag = PR[:, n % 2, :, :].rearrange("p c (b s) -> p c b s", s=HALF)[:, :, 0:tiles, 0:P]
                signal(e.affine_select(out=diag, in_=diag, compare_op=ALU.is_ge, fill=0.0, base=0,
                                       pattern=[[0, 4], [0, tiles], [1, P]], channel_multiplier=-1), "d_mk")

        def u_pv(en, e, beta, par, k, bank, prev):
            g, seg = divmod(k, 3)
            if en == "pe":
                if k == 0:
                    after(e, "d_v", beta, 1)
                if seg == 0:
                    after(e, "d_ov", beta, g - 1)
                after(e, "d_mk", beta, k)
                for j, at, w in segment_offsets(seg):
                    for c in range(4):
                        last = nc.tensor.matmul(PVB[32 * c:32 * c + VW, j * P:S], V[par][:, j, 4 * g + c, :],
                                                PR[:, k % 2, c, at:at + w], start=j == 0, stop=j == TT - 1)
                signal(last, "f_pv")
            elif en == "act" and seg == 2:
                wait(e, s_ost[g % 2], 32 * beta + 16 * (g // 2))
                after(e, "f_pv", beta, k)
                signal(e.activation(O[:, g % 2, :], PVB[:], ACT.Copy), "d_ov")
            elif en == "sp" and seg == 2:
                wait(e, s_oc[g // 2], 32 * beta)
                after(e, "d_ov", beta, g)
                e.dma_start(scratch_o[g * P:(g + 1) * P, :], O[:, g % 2, :]).then_inc(s_ost[g % 2], 16)

        def heads8(k):
            return scratch_o[k * 2 * P:(k + 1) * 2 * P, :].rearrange("(h r) s -> h r s", r=32)

        def u_od(en, e, beta, par, k, bank, prev):
            if en == "sp":
                for m in range(2):
                    wait(e, s_ost[m], 32 * beta + 16 * (k + 1))
                after(e, "d_ol", beta, k - 1)
                e.dma_start(SUMS[:], heads8(k)[:, D, :].rearrange("h (a s) -> h a s", s=64)).then_inc(s_sum, 16)
                e.dma_start(OC[:], heads8(k)[:, 0:D, :]).then_inc(s_oc[k], 16)

        def u_or(en, e, beta, par, k, bank, prev):
            if en == "dve":
                wait(e, s_sum, 32 * beta + 16 * (k + 1))
                signal(e.reciprocal(RSUMS[:], SUMS[:]), "d_rc")
            elif en == "sp":
                after(e, "d_rc", beta, k)
                e.dma_start(scratch_r[k].rearrange("h (a s) -> (h a) s", s=64), RSUMS[:]).then_inc(s_rst, 16)

        def u_ob(en, e, beta, par, k, bank, prev):
            if en == "sp":
                wait(e, s_rst, 32 * beta + 16 * (k + 1))
                e.dma_start(RDEN[:], scratch_r[k].rearrange("h (o s) -> h o s", o=1).to_broadcast([8, D, S])).then_inc(s_oc[k], 16)

        def u_on(en, e, beta, par, k, bank, prev):
            if en == "pool":
                wait(e, s_oc[k], 32 * (beta + 1))
                signal(e.tensor_tensor(OC[:], OC[:], RDEN[:], ALU.mult), "d_on")

        def u_os(en, e, beta, par, k, bank, prev):
            if en == "act":
                after(e, "d_on", beta, k)
                signal(e.activation(r(OT[0][:, k, :]), OC[:], ACT.Copy), "d_oh")
            elif en == "dve":
                after(e, "d_oh", beta, k)
                signal(e.tensor_tensor(r(OT[1][:, k, :]), OC[:], OT[0][:, k, :], ALU.subtract), "d_ol")

        def u_op(en, e, beta, par, k, bank, prev):
            if en == "pe":
                after(e, "d_ol", beta, 1)
                prev(e)
                for kt in range(KT):
                    last = parts_product(bank[:, 0:E], [part[:, kt, k * P:(k + 1) * P] for part in OT],
                                         [part[:, kt, :] for part in W["o"]], kt == 0, kt == KT - 1)
                signal(last, "f_op")
            elif en == "dve":
                after(e, "f_op", beta, k)
                after(e, "d_fin", beta, max(k - 2, -1))
                signal(e.scalar_tensor_tensor(out=Y[:, k % 2, :], in0=bank[:, 0:E], scalar=0.5 * SCALE_W, in1=G[par][:, k, :],
                                              op0=ALU.mult, op1=ALU.mult), "d_y")
            elif en == "pool":
                after(e, "d_y", beta, k)
                if k == 0:
                    wait(e, s_xc, 16 * (beta + 1))
                signal(e.tensor_tensor(X[par][:, k, :], Y[:, k % 2, :], X[par][:, k, :], ALU.add), "d_fin")
            elif en == "sp" and k % 2:
                after(e, "d_fin", beta, k)
                e.dma_start(out[beta].rearrange("(t p) e -> p t e", p=P)[:, k - 1:k + 1, :],
                            X[par][:, k - 1:k + 1, :]).then_inc(s_out, 16)

        def u_wt(en, e, beta, par, k, bank, prev):
            w, src, stage, free = WEIGHTS[k]
            if en == "sp":
                wait(e, c_wl, free)
                dst = stage if src.dtype == FP32 else stage.bitcast(INT32)
                e.dma_start(dst.rearrange("p (t n) -> p t n", t=src.shape[0] // P),
                            src.rearrange("(t p) n -> p t n", p=P)).then_inc(s_w[w], 16)
            elif en == "act":
                if src.dtype == FP32:
                    e.wait_ge(s_w[w], 16)
                else:
                    e.wait_ge(c_wf, "gud".index(w) + 1)
                e.activation(r(W[w][0][:]).rearrange("p t n -> p (t n)"), stage, ACT.Copy).then_inc(c_wh, 1)
            elif en == "dve":
                e.wait_ge(s_w[w], 16)
                if src.dtype != FP32:
                    e.tensor_copy(stage, stage.bitcast(INT32)).then_inc(c_wf, 1)
                e.wait_ge(c_wh, k + 1)
                e.tensor_tensor(r(W[w][1][:]).rearrange("p t n -> p (t n)"), stage,
                                W[w][0][:].rearrange("p t n -> p (t n)"), ALU.subtract).then_inc(c_wl, 1)

        def u_fl(en, e, beta, par, k, bank, prev):
            if en == "dve" and k == 0:
                e.wait_ge(c_wl, len(W))
                for i, w in enumerate("gud"):
                    e.tensor_reduce(LOW[:, i:i + 1], W[w][1][:].rearrange("p t n -> p (t n)"), axis=AX.X, op=ALU.max,
                                    apply_absolute_value=True).then_inc(s_flag, 1)
                e.wait_ge(s_flag, 3)
                e.tensor_reduce(LOW[:, 3:4], LOW[:, 0:3], axis=AX.X, op=ALU.max).then_inc(s_flag, 1)
            elif en == "dve":
                e.wait_ge(s_flag, 5)
                e.tensor_reduce(LOW1[:], bank[0:1, 0:P], axis=AX.X, op=ALU.max).then_inc(s_flag, 1)
                e.wait_ge(s_flag, 6)
                e.tensor_scalar(FLAG[:], LOW1[:], 0.0, None, ALU.is_gt).then_inc(s_flag, 1)
            elif en == "pe" and k == 1:
                e.wait_ge(s_flag, 4)
                e.transpose(bank[0:1, 0:P], LOW[:, 3:4], IDF[:]).then_inc(s_flag, 1)

        UNIT = dict(wt=u_wt, ld=u_ld, la=u_la, lb=u_lb, tr=u_tr, qk=u_qk, ls=u_ls, v=u_v, gu=u_gu, hs=u_hs, fl=u_fl, dn=u_dn, sm=u_sm,
                    mt=u_mt, st=u_st, pv=u_pv, od=u_od, ob=u_ob, on=u_on, os=u_os, op=u_op, xc=u_xc)
        UNIT["or"] = u_or

        def step(en, e, b, parity, units, users):
            for kind, ahead, k, n in units:
                def prev(e, n=n):
                    if n in users:
                        last, last_ahead, last_k = users[n]
                        after(e, RELEASED[last], b + last_ahead, last_k)
                UNIT[kind](en, e, b + ahead, (parity + ahead) % 2, k, None if n is None else BANKS[n], prev)
                if n is not None:
                    users[n] = (kind, ahead, k)
            return {n: (kind, ahead - 1, k) for n, (kind, ahead, k) in users.items()}

        stage_p = PR[:].rearrange("p a b c -> p (a b c)")
        stage_g = GATES[:].rearrange("p a t e -> p (a t e)")
        WEIGHTS = [
            ("k", wkT, stage_p[:, 0:512], 0), ("q", wqT, stage_p[:, 512:1024], 0), ("v", wvT, stage_p[:, 1024:1536], 0),
            ("g", wgT, stage_p[:, 1536:3072], 0), ("u", wuT, stage_g[:, 0:1536], 0),
            ("o", woT, stage_p[:, 3072:3584], 0), ("d", wdT, stage_p[:, 0:1536], 3)]
        ORDER = [w for w, *_ in WEIGHTS]

        def first_step(en, e):
            for kind in ("ld", "la", "lb"):
                UNIT[kind](en, e, 0, 0, 0, None, None)
            if en == "pool":
                for v in V:
                    e.memset(v[:], 1.0).then_inc(s_const, 1)
                for i in range(2):
                    e.memset(KS[i][:], 1.0).then_inc(s_const, 1)
                    e.memset(QS[i][:], 0.0).then_inc(s_const, 1)
            for k in ((0, 1, 2, 3, 4, 5) if en == "sp" else (0, 1, 2)):
                u_wt(en, e, 0, 0, k, None, None)
            if en == "sp":
                e.wait_ge(s_const, 12)
            units = [u for u in schedule(1, last=False, current=False) if u[0] != "lb"]
            at = {(kind, k): i for i, (kind, _, k, _) in enumerate(units)}
            before = {at["v", 0]: ("wt", (3, 4)), at["sm", 16]: ("wt", (5, 6)), at["mt", 0]: ("fl", (0,))}
            users, start = {}, 0
            for i in sorted(before):
                users = step(en, e, -1, 1, units[start:i], users)
                users = {n: (kind, ahead + 1, k) for n, (kind, ahead, k) in users.items()}
                if i == at["v", 0]:
                    if en == "act":
                        e.wait_ge(s_const, 10)
                    if en == "sp":
                        u_wt(en, e, 0, 0, 6, None, None)
                kind, ks = before[i]
                for k in ks:
                    if en != "sp":
                        UNIT[kind](en, e, 0, 0, k, None, None)
                start = i
            users = step(en, e, -1, 1, units[start:], users)
            u_fl(en, e, 0, 0, 1, PVB, None)
            return users

        def later_steps(en, e, users):
            users = step(en, e, 0, 0, schedule(0, last=False), users)
            with e.Fori(0, LOOPS) as pair:
                b = 2 * pair + 1
                after_one = step(en, e, b, 1, schedule(1), dict(users))
                step(en, e, b + 1, 0, schedule(0), after_one)
            for b in range(2 * LOOPS + 1, B + 1):
                ends = schedule(b % 2, current=b < B, following=b + 1 < B, after_next=b + 2 < B)
                users = step(en, e, b, b % 2, ends, users)

        def run(en, e):
            users = first_step(en, e)
            if en == "sp":
                e.wait_ge(s_const, 14)
            if en in ("act", "sp"):
                wait(e, c_wl, len(W))
            if en != "pe":
                later_steps(en, e, users)
                return
            e.wait_ge(s_const, 14)
            e.wait_ge(s_flag, 7)
            large = e.value_load(FLAG[0:1, 0:1], min_val=0, max_val=1)
            with e.If(large):
                short[0] = False
                later_steps(en, e, dict(users))
            with e.Else():
                short[0] = True
                later_steps(en, e, dict(users))

        block = ctx.enter_context(nc.Block())

        @block.gpsimd
        def _(e):
            e.memset(IDF[:], 0.0).then_inc(s_const, 1)
            e.memset(IDB[:], 0.0).then_inc(s_const, 1)
            e.memset(MASK[:], 0.0).then_inc(s_const, 1)
            e.memset(ZERO[:], 0.0).then_inc(s_const, 1)
            e.memset(MINUS_HALF[:], -0.5).then_inc(s_const, 1)
            e.wait_ge(s_const, 5)
            for m in (IDF, IDB):
                e.affine_select(out=m[:], in_=m[:], compare_op=ALU.not_equal, fill=1.0, base=0,
                                pattern=[[-1, P]], channel_multiplier=1).then_inc(s_const, 1)
            e.affine_select(out=MASK[:], in_=MASK[:], compare_op=ALU.is_ge, fill=MASKED, base=0,
                            pattern=[[0, 4], [-1, P]], channel_multiplier=1).then_inc(s_const, 1)
            run("pool", e)

        @block.sync
        def _(e):
            run("sp", e)
            e.wait_ge(s_out, 32 * B)

        @block.scalar
        def _(e):
            run("act", e)

        @block.vector
        def _(e):
            run("dve", e)

        @block.tensor
        def _(e):
            e.wait_ge(s_const, 8)
            nc.tensor.matmul(PVB[:], ZERO[:, 0:P], ZERO[:], start=True, stop=True).then_inc(s_fixed, 1)
            run("pe", e)


_IN = [("x", "L0_attn_x"), ("wqT", "L0_attn_Wq"), ("wkT", "L0_attn_Wk"), ("wvT", "L0_attn_Wv"), ("woT", "L0_attn_Wo"),
       ("wgT", "L0_ffn_w_gate"), ("wuT", "L0_ffn_w_up"), ("wdT", "L0_ffn_w_down")]


def kernel(**inputs):
    import numpy as np
    import concourse.bacc as bacc
    from concourse.bass_utils import run_bass_kernel_spmd

    nc = bacc.Bacc("TRN2", target_bir_lowering=False, num_devices=1, dynamic_dma_scratch_size=1024)
    arrays, args = {}, []
    for name, source in _IN:
        a = np.asarray(inputs[source])
        a = np.ascontiguousarray(a if name == "x" else a.T)
        arrays[name] = a
        args.append(nc.dram_tensor(name, a.shape, mybir.dt.from_np(a.dtype), kind="ExternalInput").ap())
    out = nc.dram_tensor("out", [B, S, E], FP32, kind="ExternalOutput").ap()
    scratch_qk = nc.dram_tensor("scratch_qk", [2, 2, E, S], FP32).ap()
    scratch_o = nc.dram_tensor("scratch_o", [H * 32, S], FP32).ap()
    scratch_r = nc.dram_tensor("scratch_r", [KT, 8, S], FP32).ap()
    build(nc, *args, out, scratch_qk, scratch_o, scratch_r)
    r = run_bass_kernel_spmd(nc, [arrays], core_ids=[0])
    return r.results[0]["out"]
```
